# Optimizing a Trainium2 kernel written in Bass

```python
import numpy as np
import jax
import jax.numpy as jnp

def _softmax(x, axis=-1):
    return jax.nn.softmax(x, axis=axis)

def _gelu(x):
    return jax.nn.gelu(x, approximate=True)

def _silu(x):
    return jax.nn.silu(x)

def _sigmoid(x):
    return jax.nn.sigmoid(x)

def _layernorm(x, axis=-1, eps=1e-05):
    m = jnp.mean(x, axis=axis, keepdims=True)
    v = jnp.var(x, axis=axis, keepdims=True)
    return (x - m) / jnp.sqrt(v + eps)

def _scatter_add(tgt, idx, src, axis=0):
    return tgt.at[idx].add(src)

def _segment_sum(src, seg, n):
    return jax.ops.segment_sum(src, seg, n)
kernel_name = 'mk_sandwich_d2_jaxref_r8_407d20'

def setup_inputs(seed: int=0):
    np.random.seed(seed)
    _w = jnp.asarray

    def _L0_attn_setup():
        import jax, jax.numpy as jnp
        import numpy as np
        B, N, D, H = (2, 256, 128, 16)
        HD = D // H
        SCALING = (D / H) ** 0.5
        EPS = 1e-05
        key = jax.random.key(seed)
        k1, k2, k3 = jax.random.split(key, 3)
        return {'z': jax.random.normal(k1, (B, N, D), dtype=jnp.float32), 'ln_scale': jnp.ones((D,), dtype=jnp.float32), 'ln_bias': jnp.zeros((D,), dtype=jnp.float32), 'w_qkv': jax.random.normal(k2, (D, 3 * D), dtype=jnp.float32) * D ** (-0.5), 'w_proj': jax.random.normal(k3, (D, D), dtype=jnp.float32) * D ** (-0.5), 'b_proj': jnp.zeros((D,), dtype=jnp.float32)}
    _L0_attn_in = _L0_attn_setup()

    def _L0_ffn_setup():
        import jax, jax.numpy as jnp
        import numpy as np
        FEATURES = 128
        D_IN = 128

        def fp8_gemm_optimized(x, input_scale, kernel, kernel_scale):
            s_in = input_scale[0]
            s_k = kernel_scale[0]
            x_q = (x.astype(jnp.float32) / s_in).astype(jnp.float8_e4m3fn)
            k_q = (kernel.astype(jnp.float32) / s_k).astype(jnp.float8_e4m3fn)
            y = jnp.dot(x_q.astype(jnp.float32), k_q.astype(jnp.float32), preferred_element_type=jnp.float32)
            return y * (s_in * s_k)
        key = jax.random.key(seed)
        kx, kk, kb = jax.random.split(key, 3)
        x = jax.random.normal(kx, (4, 1024, D_IN), dtype=jnp.float32)
        limit = np.sqrt(6.0 / (D_IN + FEATURES)).astype(np.float32)
        kernel = jax.random.uniform(kk, (D_IN, FEATURES), dtype=jnp.float32, minval=-limit, maxval=limit).astype(jnp.bfloat16)
        input_scale = jnp.ones((1,), dtype=jnp.float32)
        kernel_scale = jnp.ones((1,), dtype=jnp.float32)
        bias = jnp.zeros((FEATURES,), dtype=jnp.bfloat16)
        return {'x': x, 'kernel': kernel, 'input_scale': input_scale, 'kernel_scale': kernel_scale, 'bias': bias}
    _L0_ffn_in = _L0_ffn_setup()

    def _L1_attn_setup():
        import jax, jax.numpy as jnp
        import numpy as np
        from jax import lax
        DIM = 128
        EXP = 2
        GMLP_EXP = 2
        K = 4
        HID = DIM * EXP
        GHID = DIM * GMLP_EXP
        ALPHA_LOG_SCALE = -8.0

        def init_forget_gate(size, a=0.001, b=0.1, lo=-9.0, hi=-4.323):
            x = np.log(np.expm1(np.linspace(a, b, size, dtype=np.float64)))
            x = (x - x.min()) / (x.max() - x.min())
            x = x * abs(hi - lo) + lo
            return jnp.asarray(x, dtype=jnp.float32)

        def _rmsnorm(x, gamma):
            n = jnp.sqrt(jnp.sum(x * x, axis=-1, keepdims=True))
            return gamma * jnp.sqrt(jnp.float32(x.shape[-1])) * (x / n)

        def _linear_recurrence(alpha, x):

            def combine(e1, e2):
                a1, b1 = e1
                a2, b2 = e2
                return (a1 * a2, a2 * b1 + b2)
            _, h = lax.associative_scan(combine, (alpha, x), axis=1)
            return h

        def _hawk_block(x, W_in, conv_w, conv_b, W_gates, b_gates, forget_base, W_out, gamma1, gamma2, W_grow, W_shrink):
            B, T, _ = x.shape
            xn = _rmsnorm(x, gamma1)
            z = xn @ W_in.T
            gate, xc = (z[..., :HID], z[..., HID:])
            xc_t = jnp.pad(xc.transpose(0, 2, 1), ((0, 0), (0, 0), (K - 1, 0)))
            xc = lax.conv_general_dilated(xc_t, conv_w, window_strides=(1,), padding='VALID', dimension_numbers=('NCH', 'OIH', 'NCH'), feature_group_count=HID)
            xc = (xc + conv_b[None, :, None]).transpose(0, 2, 1)
            g = xc @ W_gates.T + b_gates
            forget, inp = (g[..., :HID], g[..., HID:])
            alpha = jnp.exp(ALPHA_LOG_SCALE * jax.nn.softplus(forget_base) * jax.nn.sigmoid(forget))
            beta = jnp.sqrt(1.0 - alpha ** 2 + 1e-06)
            xs = beta * jax.nn.sigmoid(inp) * xc
            h = _linear_recurrence(alpha, xs)
            rglru_out = jax.nn.gelu(gate, approximate=False) * h @ W_out.T
            x = x + rglru_out
            xn2 = _rmsnorm(x, gamma2)
            gz = xn2 @ W_grow.T
            mgate, mx = (gz[..., :GHID], gz[..., GHID:])
            mlp_out = jax.nn.gelu(mgate, approximate=False) * mx @ W_shrink.T
            return x + mlp_out
        key = jax.random.key(seed)
        ks = jax.random.split(key, 10)
        B, T = (4, 256)
        x = jax.random.normal(ks[0], (B, T, DIM), dtype=jnp.float32)
        W_in = jax.random.normal(ks[1], (2 * HID, DIM), dtype=jnp.float32) * DIM ** (-0.5)
        conv_w = jax.random.normal(ks[2], (HID, 1, K), dtype=jnp.float32) * (1.0 / K) ** 0.5
        conv_b = jnp.zeros((HID,), dtype=jnp.float32)
        W_gates = jax.random.normal(ks[3], (2 * HID, HID), dtype=jnp.float32) * HID ** (-0.5)
        b_gates = jnp.zeros((2 * HID,), dtype=jnp.float32)
        forget_base = init_forget_gate(HID)
        W_out = jax.random.normal(ks[4], (DIM, HID), dtype=jnp.float32) * HID ** (-0.5)
        gamma1 = jnp.ones((DIM,), dtype=jnp.float32)
        gamma2 = jnp.ones((DIM,), dtype=jnp.float32)
        W_grow = jax.random.normal(ks[5], (2 * GHID, DIM), dtype=jnp.float32) * DIM ** (-0.5)
        W_shrink = jax.random.normal(ks[6], (DIM, GHID), dtype=jnp.float32) * GHID ** (-0.5)
        return {'x': x, 'W_in': W_in, 'conv_w': conv_w, 'conv_b': conv_b, 'W_gates': W_gates, 'b_gates': b_gates, 'forget_base': forget_base, 'W_out': W_out, 'gamma1': gamma1, 'gamma2': gamma2, 'W_grow': W_grow, 'W_shrink': W_shrink}
    _L1_attn_in = _L1_attn_setup()

    def _L1_ffn_setup():
        import jax, jax.numpy as jnp
        import numpy as np
        EXPERT_NUM = 8
        CAPACITY = 100
        key = jax.random.key(seed)
        k1, k2, k3 = jax.random.split(key, 3)
        B, S, H, E = (8, 256, 128, EXPERT_NUM)
        x = jax.random.normal(k1, (B, S, H), dtype=jnp.float32)
        w_gate = jax.random.normal(k2, (H, E), dtype=jnp.float32) * 0.02
        w_expert = jax.random.normal(k3, (H, H), dtype=jnp.float32) * 0.02
        b_expert = jnp.zeros((H,), dtype=jnp.float32)
        return {'x': x, 'w_gate': w_gate, 'w_expert': w_expert, 'b_expert': b_expert}
    _L1_ffn_in = _L1_ffn_setup()
    _d = {'L0_attn_z': _L0_attn_in['z'], 'L0_attn_ln_scale': _L0_attn_in['ln_scale'], 'L0_attn_ln_bias': _L0_attn_in['ln_bias'], 'L0_attn_w_qkv': _L0_attn_in['w_qkv'], 'L0_attn_w_proj': _L0_attn_in['w_proj'], 'L0_attn_b_proj': _L0_attn_in['b_proj'], 'L0_ffn_kernel': _L0_ffn_in['kernel'], 'L0_ffn_input_scale': _L0_ffn_in['input_scale'], 'L0_ffn_kernel_scale': _L0_ffn_in['kernel_scale'], 'L0_ffn_bias': _L0_ffn_in['bias'], 'L1_attn_W_in': _L1_attn_in['W_in'], 'L1_attn_conv_w': _L1_attn_in['conv_w'], 'L1_attn_conv_b': _L1_attn_in['conv_b'], 'L1_attn_W_gates': _L1_attn_in['W_gates'], 'L1_attn_b_gates': _L1_attn_in['b_gates'], 'L1_attn_forget_base': _L1_attn_in['forget_base'], 'L1_attn_W_out': _L1_attn_in['W_out'], 'L1_attn_gamma1': _L1_attn_in['gamma1'], 'L1_attn_gamma2': _L1_attn_in['gamma2'], 'L1_attn_W_grow': _L1_attn_in['W_grow'], 'L1_attn_W_shrink': _L1_attn_in['W_shrink'], 'L1_ffn_w_gate': _L1_ffn_in['w_gate'], 'L1_ffn_w_expert': _L1_ffn_in['w_expert'], 'L1_ffn_b_expert': _L1_ffn_in['b_expert']}
    _x0 = _d['L0_attn_z']
    _d['L0_attn_z'] = jax.random.normal(jax.random.fold_in(jax.random.key(seed), 1), (16, 512, 128), dtype=_x0.dtype)
    del _x0
    return _d

def reference(L0_attn_z, L0_attn_ln_scale, L0_attn_ln_bias, L0_attn_w_qkv, L0_attn_w_proj, L0_attn_b_proj, L0_ffn_kernel, L0_ffn_input_scale, L0_ffn_kernel_scale, L0_ffn_bias, L1_attn_W_in, L1_attn_conv_w, L1_attn_conv_b, L1_attn_W_gates, L1_attn_b_gates, L1_attn_forget_base, L1_attn_W_out, L1_attn_gamma1, L1_attn_gamma2, L1_attn_W_grow, L1_attn_W_shrink, L1_ffn_w_gate, L1_ffn_w_expert, L1_ffn_b_expert):

    def _L0_attn_ref(z, ln_scale, ln_bias, w_qkv, w_proj, b_proj):
        import jax, jax.numpy as jnp
        import numpy as np
        B, N, D, H = (2, 256, 128, 16)
        HD = D // H
        SCALING = (D / H) ** 0.5
        EPS = 1e-05
        b, n, d = z.shape
        mu = jnp.mean(z, axis=-1, keepdims=True)
        var = jnp.mean(jnp.square(z - mu), axis=-1, keepdims=True)
        zn = (z - mu) / jnp.sqrt(var + EPS) * ln_scale + ln_bias
        qkv = zn @ w_qkv
        qkv5 = qkv.reshape(b, n, H, HD, 3)
        q = jnp.transpose(qkv5[..., 0], (0, 2, 1, 3))
        k = jnp.transpose(qkv5[..., 1], (0, 2, 1, 3))
        v = jnp.transpose(qkv5[..., 2], (0, 2, 1, 3))
        scores = jnp.einsum('bhqd,bhkd->bhqk', q, k) / SCALING
        att = jax.nn.softmax(scores, axis=-1)
        out = jnp.einsum('bhal,bhlv->bhav', att, v)
        out = jnp.transpose(out, (0, 2, 1, 3)).reshape(b, n, d)
        out = out @ w_proj + b_proj
        return z + out

    def _L0_ffn_ref(x, kernel, input_scale, kernel_scale, bias):
        import jax, jax.numpy as jnp
        import numpy as np
        FEATURES = 128
        D_IN = 128

        def fp8_gemm_optimized(x, input_scale, kernel, kernel_scale):
            s_in = input_scale[0]
            s_k = kernel_scale[0]
            x_q = (x.astype(jnp.float32) / s_in).astype(jnp.float8_e4m3fn)
            k_q = (kernel.astype(jnp.float32) / s_k).astype(jnp.float8_e4m3fn)
            y = jnp.dot(x_q.astype(jnp.float32), k_q.astype(jnp.float32), preferred_element_type=jnp.float32)
            return y * (s_in * s_k)
        dtype = jnp.bfloat16
        x = x.astype(dtype)
        orig_shape = x.shape
        x2 = x.reshape(-1, x.shape[-1])
        y = fp8_gemm_optimized(x2, input_scale, kernel, kernel_scale)
        y = y.astype(dtype) + bias
        return y.reshape(orig_shape[:-1] + (FEATURES,))

    def _L1_attn_ref(x, W_in, conv_w, conv_b, W_gates, b_gates, forget_base, W_out, gamma1, gamma2, W_grow, W_shrink):
        import jax, jax.numpy as jnp
        import numpy as np
        from jax import lax
        DIM = 128
        EXP = 2
        GMLP_EXP = 2
        K = 4
        HID = DIM * EXP
        GHID = DIM * GMLP_EXP
        ALPHA_LOG_SCALE = -8.0

        def init_forget_gate(size, a=0.001, b=0.1, lo=-9.0, hi=-4.323):
            x = np.log(np.expm1(np.linspace(a, b, size, dtype=np.float64)))
            x = (x - x.min()) / (x.max() - x.min())
            x = x * abs(hi - lo) + lo
            return jnp.asarray(x, dtype=jnp.float32)

        def _rmsnorm(x, gamma):
            n = jnp.sqrt(jnp.sum(x * x, axis=-1, keepdims=True))
            return gamma * jnp.sqrt(jnp.float32(x.shape[-1])) * (x / n)

        def _linear_recurrence(alpha, x):

            def combine(e1, e2):
                a1, b1 = e1
                a2, b2 = e2
                return (a1 * a2, a2 * b1 + b2)
            _, h = lax.associative_scan(combine, (alpha, x), axis=1)
            return h

        def _hawk_block(x, W_in, conv_w, conv_b, W_gates, b_gates, forget_base, W_out, gamma1, gamma2, W_grow, W_shrink):
            B, T, _ = x.shape
            xn = _rmsnorm(x, gamma1)
            z = xn @ W_in.T
            gate, xc = (z[..., :HID], z[..., HID:])
            xc_t = jnp.pad(xc.transpose(0, 2, 1), ((0, 0), (0, 0), (K - 1, 0)))
            xc = lax.conv_general_dilated(xc_t, conv_w, window_strides=(1,), padding='VALID', dimension_numbers=('NCH', 'OIH', 'NCH'), feature_group_count=HID)
            xc = (xc + conv_b[None, :, None]).transpose(0, 2, 1)
            g = xc @ W_gates.T + b_gates
            forget, inp = (g[..., :HID], g[..., HID:])
            alpha = jnp.exp(ALPHA_LOG_SCALE * jax.nn.softplus(forget_base) * jax.nn.sigmoid(forget))
            beta = jnp.sqrt(1.0 - alpha ** 2 + 1e-06)
            xs = beta * jax.nn.sigmoid(inp) * xc
            h = _linear_recurrence(alpha, xs)
            rglru_out = jax.nn.gelu(gate, approximate=False) * h @ W_out.T
            x = x + rglru_out
            xn2 = _rmsnorm(x, gamma2)
            gz = xn2 @ W_grow.T
            mgate, mx = (gz[..., :GHID], gz[..., GHID:])
            mlp_out = jax.nn.gelu(mgate, approximate=False) * mx @ W_shrink.T
            return x + mlp_out
        return _hawk_block(x, W_in, conv_w, conv_b, W_gates, b_gates, forget_base, W_out, gamma1, gamma2, W_grow, W_shrink)

    def _L1_ffn_ref(x, w_gate, w_expert, b_expert):
        import jax, jax.numpy as jnp
        import numpy as np
        EXPERT_NUM = 8
        CAPACITY = 100
        B, S, H = x.shape
        E, C = (EXPERT_NUM, CAPACITY)
        hs = x.reshape(-1, H)
        logits = hs @ w_gate
        probs = jax.nn.softmax(logits, axis=1)
        best = jnp.argmax(probs, axis=1)
        mask = jax.nn.one_hot(best, E, dtype=jnp.int32)
        gate = jnp.sum(probs * mask.astype(probs.dtype), axis=1)
        locations = jnp.cumsum(mask, axis=0) - 1
        mask = mask * (locations < C).astype(jnp.int32)
        loc_sum = jnp.sum(locations * mask, axis=1)
        new_gates = gate[:, None] * mask.astype(probs.dtype)
        loc_oh = jax.nn.one_hot(loc_sum, C, dtype=probs.dtype)
        combine = new_gates[:, :, None] * loc_oh[:, None, :]
        dispatch = (combine != 0).astype(hs.dtype)
        dispatched = jnp.einsum('tec,th->ech', dispatch, hs).reshape(E * C, H)
        expert_out = dispatched @ w_expert + b_expert
        combined = combine.reshape(-1, E * C) @ expert_out
        return combined.reshape(B, S, H)
    x = L0_attn_z
    x = x + _layernorm(_L0_attn_ref(_layernorm(x, axis=-1), L0_attn_ln_scale, L0_attn_ln_bias, L0_attn_w_qkv, L0_attn_w_proj, L0_attn_b_proj), axis=-1)
    x = x + _layernorm(_L0_ffn_ref(_layernorm(x, axis=-1), L0_ffn_kernel, L0_ffn_input_scale, L0_ffn_kernel_scale, L0_ffn_bias), axis=-1)
    x = x + _layernorm(_L1_attn_ref(_layernorm(x, axis=-1), L1_attn_W_in, L1_attn_conv_w, L1_attn_conv_b, L1_attn_W_gates, L1_attn_b_gates, L1_attn_forget_base, L1_attn_W_out, L1_attn_gamma1, L1_attn_gamma2, L1_attn_W_grow, L1_attn_W_shrink), axis=-1)
    x = x + _layernorm(_L1_ffn_ref(_layernorm(x, axis=-1), L1_ffn_w_gate, L1_ffn_w_expert, L1_ffn_b_expert), axis=-1)
    return x

_drawn_inputs = setup_inputs


def setup_inputs(seed=0):
    import zlib

    import numpy as np

    out = dict(_drawn_inputs(seed))
    spreads = {'L0_attn_ln_scale': (1.0, 0.2),
     'L0_attn_ln_bias': (0.0, 0.1),
     'L0_attn_b_proj': (0.0, 0.1),
     'L0_ffn_bias': (0.0, 0.1),
     'L1_attn_conv_b': (0.0, 0.1),
     'L1_attn_b_gates': (0.0, 0.682),
     'L1_attn_gamma1': (1.0, 0.2),
     'L1_attn_gamma2': (1.0, 0.2),
     'L1_ffn_b_expert': (0.0, 0.1)}
    factors = {}
    for name, (base, spread) in spreads.items():
        noise = np.random.default_rng([zlib.crc32(name.encode()), seed]).standard_normal(out[name].shape)
        drawn = base * np.exp(spread * noise) if base else spread * noise
        out[name] = jnp.asarray(drawn.astype(out[name].dtype))
    for name, factor in factors.items():
        out[name] = (out[name] * factor).astype(out[name].dtype)
    return out
```

```python
from contextlib import ExitStack

import concourse.bass as bass
from concourse import mybir

ALU = mybir.AluOpType
ACT = mybir.ActivationFunctionType
AX_X = mybir.AxisListType.X
F32 = mybir.dt.float32
BF16 = mybir.dt.bfloat16
U32 = mybir.dt.uint32

P = 128
D = 128
EPS = 1e-5


def wait(eng, sem, value):
    if isinstance(value, int):
        if value > 0:
            eng.wait_ge(sem, value)
    else:
        eng.wait_ge(sem, value)


def wait_apart(eng, sem, value, past_wait):
    wait(eng, sem, value)
    if not isinstance(value, int):
        eng.sem_inc(past_wait, 1)


def bank_free(pe, i, live, uses, name):
    at = [u[0] for u in uses].index(name)
    for back in range(1, len(uses) * 4):
        j, n = (at - back) // len(uses), (at - back) % len(uses)
        _, off, read, per_batch, nth = uses[n]
        if live(i + j, off):
            wait(pe, read, per_batch * (i + j + off) + nth)
            return
        if isinstance(i, int) and i + j < -3:
            return


def norm_stats(nc, dve, src, bn, mv, raw, done, C, b, past_wait):
    for c in range(C):
        nc.vector.bn_stats(bn[:, c, :], src(c)).then_inc(raw, 1)
    wait_apart(dve, raw, C * (b + 1), past_wait)
    for c in range(C):
        nc.vector.bn_aggr(mv[:, c, :], bn[:, c, :]).then_inc(done, 1)


def attention_phase(nc, ctx, sems, psum, x_in, x_all, w, consts, NB):
    C = x_in.shape[1] // P
    T = x_in.shape[1]
    H, HD = 16, 8
    NP = H // 2
    SPLIT = 6
    Q_PART = (0, 0, 0, 1, 1, 2)
    K_PART = (0, 1, 2, 0, 1, 0)
    KROWS = SPLIT * HD
    MROWS = 3
    SCALE = float(1.0 / (D / H) ** 0.5)
    STACK_DMAS = 3 * SPLIT
    KSTACK_DMAS = SPLIT
    MROW_DMAS = 2

    def sb(name, shape, dt=F32):
        return ctx.enter_context(nc.sbuf_tensor(name, shape, dt))

    def sem(name):
        return ctx.enter_context(nc.semaphore(name))

    q_stack = [sb(f"q_stack{i}", [P, NP, T], BF16) for i in range(2)]
    k_stack = [sb(f"k_stack{i}", [P, NP, T], BF16) for i in range(2)]
    v_pad = [sb(f"v_pad{i}", [P, C, H, 32]) for i in range(2)]
    probs = sb("probs", [P, 2 * 4 * C, T])
    q_parts = sb("q_parts", [P, 3, T], BF16)
    k_parts = sb("k_parts", [P, 3, T], BF16)
    q_rest = sb("q_rest", [P, T])
    k_rest = sb("k_rest", [P, T])
    neg_max = [sb(f"neg_max{i}", [P, C, 4, 2]) for i in range(2)]
    max_rest = sb("max_rest", [P, C, 2, 4])
    max_parts = sb("max_parts", [P, C, 2, 3, 4], BF16)
    max_rows = sb("max_rows", [3 * 8, T], BF16)
    bn_a = sb("bn_a", [P, C, 6])
    mv_a = sb("mv_a", [P, C, 2])
    bn_b = sb("bn_b", [P, C, 6])
    mv_b = sb("mv_b", [P, C, 2])
    bn_c = sb("bn_c", [P, C, 6])
    mv_c = sb("mv_c", [P, C, 2])
    bn_d = sb("bn_d", [P, C, 6])
    mv_d = sb("mv_d", [P, C, 2])
    mean_rs = sb("mean_rs", [P, NB, 2, C])
    tiny = sb("tiny", [P, 8, C])
    tiny_bf = sb("tiny_bf", [P, 4, C], BF16)
    centred = sb("centred", [P, C, D])
    zn = sb("zn", [P, C, D])
    znT = sb("znT", [P, T])
    outT = [sb(f"outT{i}", [P, T]) for i in range(2)]
    rowsum_inv = sb("rowsum_inv", [P, C * 4 * 2])
    o_nat = sb("o_nat", [P, C, 2, 8, HD])
    oT = sb("oT", [P, T])
    z_res = sb("z_res", [P, C, D])
    att = sb("att", [P, C, D])
    att_c = centred
    y_bf = sb("y_bf", [P, C, D], BF16)
    y_scaled = sb("y_scaled", [P, C * D])
    y_grid = sb("y_grid", [P, C * D])
    y_sum = sb("y_sum", [P, C * D])
    y_q = sb("y_q", [P, C, D], BF16)
    y_absmax = sb("y_absmax", [P, C])
    poison = sb("poison", [P, C])
    yT = sb("yT", [P, T], BF16)
    f_bf = sb("f_bf", [P, C, D], BF16)
    f_b = sb("f_b", [P, C, D], BF16)
    f_c = sb("f_c", [P, C, D], BF16)

    score_ps = psum[0:2]
    st_ps = psum[2:4]
    acc = psum[4]
    misc = psum[5]
    misc_bf = misc[:, 0:T // 2].bitcast(BF16)

    x_loaded, past_wait = sems["x_loaded"], sems["past_wait"]
    names = ("stat_a stat_a_raw prep_step zn_ready znT_ps znT_ready q_ps q_hi q_r q_lo k_ps k_hi k_r k_lo "
             "stack_ready kstack_ready max_ps max_read max_split maxT_ps maxT_read mrow_ready st_ready exp_done pv_done "
             "acc_read o_ps rowsum_ready o_nat_ready oT_ps oT_ready v_ps v_ready zres_step proj_ps att_ready "
             "stat_b_raw stat_b x1_step stat_c_raw stat_c y_step quant_step yT_ps yT_ready ffn_ps ffn_read "
             "ffn_biased stat_d_raw stat_d x2_step").split()
    s = {n: sem(n) for n in names}
    sems.update(s)

    def live(i, off):
        return not isinstance(i, int) or 0 <= i + off < NB

    MISC = [("yT", -2, s["yT_ready"], 1, 1), ("ffn", -2, s["ffn_read"], 1, 1), ("maxT1", 0, s["maxT_read"], 2, 2),
            ("o1", -1, s["o_nat_ready"], 2, 2), ("v", 1, s["v_ready"], 2, 2), ("oT", -1, s["oT_ready"], 1, 1),
            ("proj", -1, s["att_ready"], 1, 1), ("znT", 2, s["znT_ready"], 1, 1), ("q", 2, s["q_r"], 1, 1),
            ("maxT0", 1, s["maxT_read"], 2, 1), ("k", 2, s["k_r"], 1, 1), ("o0", 0, s["o_nat_ready"], 2, 1)]

    def wait_misc_free(pe, i, name):
        bank_free(pe, i, live, MISC, name)

    def tensor(pe, i, par):
        def score_max(p, c):
            j, b, bpar = (p + 6) % NP, (i if p < 2 else i + 1), (par if p < 2 else 1 - par)
            if not live(b, 0):
                return
            if j == 0 and c == 0:
                wait(pe, s["stack_ready"], 16 * STACK_DMAS * (b + 1))
                wait(pe, s["kstack_ready"], 16 * KSTACK_DMAS * (b + 1))
            wait(pe, s["max_read"], 32 * b + 4 * j + c - 1)
            for h in range(2):
                rows = slice(64 * h, 64 * h + KROWS)
                mm = nc.tensor.matmul(score_ps[c % 2][:, h, :], q_stack[bpar][rows, j, c * P:(c + 1) * P],
                                      k_stack[bpar][rows, j, :], start=True, stop=True)
            mm.then_inc(s["max_ps"], 1)

        def score_t(p, c):
            if c == 0 and p in (0, 4):
                wait(pe, s["mrow_ready"], 16 * MROW_DMAS * (2 * i + 1 + p // 4))
            for h in range(2):
                n = 64 * i + 8 * p + 2 * c + h + 1
                wait(pe, s["exp_done"], n - 2)
                rows = slice(64 * h, 64 * h + KROWS + MROWS)
                nc.tensor.matmul(st_ps[h][:, :], k_stack[par][rows, p, c * P:(c + 1) * P],
                                 q_stack[par][rows, p, :], start=True, stop=True).then_inc(s["st_ready"], 1)

        def prob_v(p, c):
            b, a, bpar = (i - 1, 3, 1 - par) if p < 2 else (i, p // 2 - 1, par)
            if not live(b, 0):
                return
            kc = 2 * (p % 2) + c // 2
            u, t = a // 2, a % 2
            if a == 0 and kc == 0:
                wait(pe, s["v_ready"], 2 * b + 2)
            if t == 0 and kc == 0:
                wait(pe, s["acc_read"], 2 * b + u)
            wait(pe, s["exp_done"], 64 * b + 8 * (2 * a + 1) + 2 * kc + 2)
            for g in range(4):
                mm = nc.tensor.matmul(acc[32 * g:32 * g + 32, :], v_pad[bpar][:, kc, 4 * a + g, :],
                                      probs[:, (a % 2) * 4 * C + g * C + kc, :],
                                      start=(t == 0 and kc == 0), stop=(t == 1 and kc == C - 1),
                                      skip_group_check=True)
            mm.then_inc(s["pv_done"], 1)

        def transpose4(src, ident, out, n, done):
            for c in range(C):
                mm = nc.tensor.transpose(out[0:n, c * P:(c + 1) * P], src(c), ident)
            mm.then_inc(done, 1)

        def max_t(half, b):
            name = f"maxT{half}"
            wait(pe, s["max_split"], 4 * (2 * b + half + 1))
            wait_misc_free(pe, i, name)
            transpose4(lambda c: max_parts[:, c].rearrange("p s a j -> p (s a j)"), consts["ident_bf"][:, :],
                       misc_bf, 3 * 8, s["maxT_ps"])

        def out_nat(u, b):
            wait(pe, s["acc_read"], 2 * b + u + 1)
            wait_misc_free(pe, i, f"o{u}")
            transpose4(lambda c: outT[u][:, c * P:(c + 1) * P], consts["ident"][:, :], misc, P, s["o_ps"])

        def side_product(slot):
            if slot == 2 and live(i, -2):
                wait(pe, s["quant_step"], 10 * (i - 2) + 5)
                wait_misc_free(pe, i, "yT")
                transpose4(lambda c: y_q[:, c, :], consts["ident_bf"][:, :], misc_bf, P, s["yT_ps"])
            if slot == 3 and live(i, -2):
                wait(pe, s["yT_ready"], i - 2 + 1)
                wait_misc_free(pe, i, "ffn")
                for c in range(C):
                    mm = nc.tensor.matmul(misc[:, c * D:(c + 1) * D], yT[:, c * P:(c + 1) * P], w["ffn"][:, :],
                                          start=True, stop=True)
                mm.then_inc(s["ffn_ps"], 1)
            if slot == 4 and live(i, 0):
                max_t(1, i)
            if slot == 5 and live(i, -1):
                out_nat(1, i - 1)
            if slot == 6 and live(i, 1):
                wait(pe, s["znT_ready"], i + 1 + 1)
                wait_misc_free(pe, i, "v")
                for c in range(C):
                    mm = nc.tensor.matmul(misc[:, c * D:(c + 1) * D], znT[:, c * P:(c + 1) * P], w["v"][:, :],
                                          start=True, stop=True)
                mm.then_inc(s["v_ps"], 1)
            if slot == 7 and live(i, -1):
                wait(pe, s["o_nat_ready"], 2 * (i - 1) + 2)
                wait_misc_free(pe, i, "oT")
                transpose4(lambda c: o_nat[:, c].rearrange("p u g d -> p (u g d)"), consts["ident"][:, :],
                           misc, P, s["oT_ps"])
            if slot == 9 and live(i, 2):
                wait(pe, s["zn_ready"], i + 2 + 1)
                wait_misc_free(pe, i, "znT")
                transpose4(lambda c: zn[:, c, :], consts["ident"][:, :], misc, P, s["znT_ps"])
            if slot == 8 and live(i, -1):
                wait(pe, s["oT_ready"], i - 1 + 1)
                wait_misc_free(pe, i, "proj")
                for c in range(C):
                    mm = nc.tensor.matmul(misc[:, c * D:(c + 1) * D], oT[:, c * P:(c + 1) * P], w["proj"][:, :],
                                          start=True, stop=True)
                mm.then_inc(s["proj_ps"], 1)
            if slot in (11, 13) and live(i, 2):
                n = "q" if slot == 11 else "k"
                wait(pe, s["znT_ready"], i + 2 + 1)
                wait_misc_free(pe, i, n)
                nc.tensor.matmul(misc[:, :], w[n][:, :], znT[:, :], start=True, stop=True).then_inc(s[n + "_ps"], 1)
            if slot == 12 and live(i, 1):
                max_t(0, i + 1)
            if slot == 14 and live(i, 0):
                out_nat(0, i)

        for p in range(NP):
            for c in range(0, C, 2):
                if live(i, 0):
                    score_t(p, c)
                score_max(p, c)
                score_max(p, c + 1)
                if live(i, 0):
                    score_t(p, c + 1)
                prob_v(p, c + 1)
                side_product(2 * p + c // 2)

    def scalar(act, i, par):
        def side_read(slot):
            if slot == 2 and live(i, -2):
                wait(act, s["yT_ps"], i - 2 + 1)
                wait(act, s["ffn_ps"], i - 2)
                nc.scalar.activation(yT[:, :], misc_bf, ACT.Copy).then_inc(s["yT_ready"], 1)
            for at, u, off in ((3, 1, -1), (11, 0, 0)):
                if slot == at and live(i, off):
                    b = i + off
                    wait(act, s["pv_done"], 16 * b + 8 * (u + 1))
                    wait(act, s["o_ps"], 2 * (b - 1) + u + 1)
                    nc.scalar.activation(outT[u][:, :], acc[:, :], ACT.Copy).then_inc(s["acc_read"], 1)
            if slot == 3 and live(i, -2):
                wait(act, s["ffn_ps"], i - 2 + 1)
                wait(act, s["ffn_biased"], i - 2)
                nc.scalar.activation(f_bf[:, :, :].rearrange("p c d -> p (c d)"), misc[:, :], ACT.Identity,
                                     bias=0.0, scale=consts["s_both"][:, 0:1]).then_inc(s["ffn_read"], 1)
            for at, half, off in ((4, 1, 0), (12, 0, 1)):
                if slot == at and live(i, off):
                    n = 2 * (i + off) + half
                    wait(act, s["maxT_ps"], n + 1)
                    wait(act, s["mrow_ready"], 16 * MROW_DMAS * n)
                    nc.scalar.activation(max_rows[:, :], misc_bf[0:3 * 8, :], ACT.Copy).then_inc(s["maxT_read"], 1)
            if slot == 6 and live(i, 1):
                wait(act, s["v_ps"], i + 1 + 1)
                wait(act, s["pv_done"], 16 * (i - 1) + 16)
                src = misc[:, :].rearrange("p (cu t g d) -> p cu t g d", t=2, g=4, d=HD)
                dst = v_pad[1 - par][:, :, :, :].rearrange("p c (u t g) e -> p (c u) t g e", u=2, t=2)
                for t in range(2):
                    nc.scalar.activation(dst[:, :, t, :, 16 * t:16 * t + HD], src[:, :, t], ACT.Copy)\
                        .then_inc(s["v_ready"], 1)
            if slot == 7 and live(i, -1):
                wait(act, s["oT_ps"], i - 1 + 1)
                wait(act, s["proj_ps"], i - 1)
                nc.scalar.activation(oT[:, :], misc[:, :], ACT.Copy).then_inc(s["oT_ready"], 1)
            if slot == 9 and live(i, 2):
                wait(act, s["znT_ps"], i + 2 + 1)
                wait(act, s["k_ps"], i + 2)
                wait(act, s["v_ps"], i + 2)
                nc.scalar.activation(znT[:, :], misc[:, :], ACT.Identity, bias=consts["ln_bias"][:, 0:1],
                                     scale=consts["ln_scale"][:, 0:1]).then_inc(s["znT_ready"], 1)
            if slot in (11, 13) and live(i, 2):
                n, parts = ("q", q_parts) if slot == 11 else ("k", k_parts)
                wait(act, s[n + "_ps"], i + 2 + 1)
                wait(act, s["stack_ready"], 16 * STACK_DMAS * (i + 2))
                wait(act, s["kstack_ready"], 16 * KSTACK_DMAS * (i + 2))
                nc.scalar.activation(parts[:, 0, :], misc[:, :], ACT.Copy).then_inc(s[n + "_hi"], 1)

        for p in range(NP):
            for c in range(C):
                if live(i, 0):
                    for h in range(2):
                        wait(act, s["st_ready"], 64 * i + 8 * p + 2 * c + h + 1)
                        wait(act, s["pv_done"], 16 * i + 4 * (p // 2) + c + 1 - 8)
                        nc.scalar.activation(probs[:, (p // 2 % 2) * 4 * C + (2 * (p % 2) + h) * C + c, :],
                                             st_ps[h][:, :], ACT.Exp, scale=SCALE).then_inc(s["exp_done"], 1)
                if c % 2:
                    side_read(2 * p + c // 2)

    def vector(dve, i, par):
        def side(slot):
            for at, half, off in ((3, 1, 0), (11, 0, 1)):
                if slot == at and live(i, off):
                    n = 2 * (i + off) + half
                    m = neg_max[half][:, :, :, :].rearrange("p c j s -> p c s j")
                    rest = max_rest[:, :, :, :]
                    wait(dve, s["max_read"], 16 * (n + 1))
                    wait(dve, s["maxT_ps"], n)
                    nc.vector.tensor_copy(max_parts[:, :, :, 0], m).then_inc(s["max_split"], 1)
                    wait(dve, s["max_split"], 4 * n + 1)
                    nc.vector.tensor_tensor(rest, m, max_parts[:, :, :, 0], ALU.subtract).then_inc(s["max_split"], 1)
                    wait(dve, s["max_split"], 4 * n + 2)
                    nc.vector.tensor_copy(max_parts[:, :, :, 1], rest).then_inc(s["max_split"], 1)
                    wait(dve, s["max_split"], 4 * n + 3)
                    nc.vector.tensor_tensor(max_parts[:, :, :, 2], rest, max_parts[:, :, :, 1], ALU.subtract)\
                        .then_inc(s["max_split"], 1)
            if slot == 2 and live(i, 2):
                b = i + 2
                wait(dve, x_loaded, 16 * (b + 1))
                wait(dve, s["prep_step"], 9 * b)
                norm_stats(nc, dve, lambda c: x_all[:, b, c * D:(c + 1) * D], bn_a, mv_a, s["stat_a_raw"], s["stat_a"], C, b, past_wait)
            for at, u, off in ((5, 1, -1), (14, 0, 0)):
                if slot == at and live(i, off):
                    n = 2 * (i + off) + u
                    o = misc[:, :].rearrange("p (g e) -> p g e", e=16)
                    wait(dve, s["o_ps"], n + 1)
                    wait(dve, s["o_nat_ready"], n)
                    nc.vector.reciprocal(rowsum_inv[:, :], o[:, :, HD:HD + 1].rearrange("p g e -> p (g e)"))\
                        .then_inc(s["rowsum_ready"], 1)
                    wait(dve, s["rowsum_ready"], n + 1)
                    wait(dve, s["oT_ps"], i + off)
                    nc.vector.tensor_tensor(
                        o_nat[:, :, u], o[:, :, 0:HD].rearrange("p (c g) d -> p c g d", c=C),
                        rowsum_inv[:, :].rearrange("p (c g) -> p c g", c=C).unsqueeze(3).to_broadcast([P, C, 8, HD]),
                        ALU.mult).then_inc(s["o_nat_ready"], 1)
            if slot == 8 and live(i, -1):
                b = i - 1
                wait(dve, s["proj_ps"], b + 1)
                wait(dve, s["zres_step"], 3 * (b + 1))
                wait(dve, s["x1_step"], 5 * b)
                nc.vector.tensor_tensor(att[:, :, :].rearrange("p c d -> p (c d)"), misc[:, :],
                                        z_res[:, :, :].rearrange("p c d -> p (c d)"), ALU.add)\
                    .then_inc(s["att_ready"], 1)
            if slot in (11, 13) and live(i, 2):
                n, parts, rest = ("q", q_parts, q_rest) if slot == 11 else ("k", k_parts, k_rest)
                wait(dve, s[n + "_hi"], i + 2 + 1)
                wait(dve, s[n + "_lo"], 2 * (i + 2))
                nc.vector.tensor_tensor(rest[:, :], misc[:, :], parts[:, 0, :], ALU.subtract)\
                    .then_inc(s[n + "_r"], 1)
            if slot == 9 and live(i, -1):
                b = i - 1
                wait(dve, s["att_ready"], b + 1)
                wait(dve, s["x1_step"], 5 * b)
                norm_stats(nc, dve, lambda c: att[:, c, :], bn_b, mv_b, s["stat_b_raw"], s["stat_b"], C, b, past_wait)
            if slot == 12 and live(i, -1):
                b = i - 1
                wait(dve, s["x1_step"], 5 * (b + 1))
                wait(dve, s["y_step"], 4 * b)
                norm_stats(nc, dve, lambda c: x_all[:, b, c * D:(c + 1) * D], bn_c, mv_c, s["stat_c_raw"], s["stat_c"], C, b, past_wait)
            q = s["quant_step"]
            if slot == 14 and live(i, -1):
                b = i - 1
                wait(dve, s["y_step"], 4 * (b + 1))
                nc.vector.tensor_scalar(y_scaled[:, :], y_bf[:, :, :].rearrange("p c d -> p (c d)"),
                                        consts["s_in_inv"][:, 0:1], None, ALU.mult).then_inc(q, 1)
            if slot == 15 and live(i, -1):
                b = i - 1
                wait(dve, q, 10 * b + 1)
                nc.vector.tensor_scalar(y_grid[:, :].bitcast(U32), y_scaled[:, :].bitcast(U32), 0x7F800000, None,
                                        ALU.bitwise_and).then_inc(q, 1)
                wait(dve, q, 10 * b + 2)
                nc.vector.tensor_scalar(y_grid[:, :], y_grid[:, :], 2.0 ** -6, 1.5 * 2.0 ** 20, ALU.max, ALU.mult)\
                    .then_inc(q, 1)
            if slot == 0 and live(i, -2):
                b = i - 2
                wait(dve, q, 10 * b + 3)
                nc.vector.tensor_tensor(y_sum[:, :], y_scaled[:, :], y_grid[:, :], ALU.add).then_inc(q, 1)
            if slot == 1 and live(i, -2):
                b = i - 2
                wait(dve, q, 10 * b + 4)
                wait(dve, s["yT_ps"], b)
                nc.vector.tensor_tensor(y_q[:, :, :].rearrange("p c d -> p (c d)"), y_sum[:, :], y_grid[:, :],
                                        ALU.subtract).then_inc(q, 1)
            if slot == 3 and live(i, -2):
                b = i - 2
                nc.vector.tensor_reduce(y_absmax[:, :], y_scaled[:, :].rearrange("p (c d) -> p c d", c=C), AX_X,
                                        ALU.max, apply_absolute_value=True).then_inc(q, 1)
                wait(dve, q, 10 * b + 6)
                nc.vector.tensor_scalar(y_absmax[:, :], y_absmax[:, :], 464.0, 464.0, ALU.max, ALU.subtract)\
                    .then_inc(q, 1)
                wait(dve, q, 10 * b + 7)
                nc.vector.tensor_scalar(y_absmax[:, :], y_absmax[:, :], 1e30, 1e30, ALU.mult, ALU.mult)\
                    .then_inc(q, 2)
                wait(dve, q, 10 * b + 9)
                wait(dve, s["x2_step"], 10 * b)
                nc.vector.tensor_scalar(poison[:, :], y_absmax[:, :], 1e30, None, ALU.mult).then_inc(q, 1)
            if slot == 4 and live(i, -2):
                b = i - 2
                wait(dve, s["ffn_read"], b + 1)
                wait(dve, s["x2_step"], 10 * b)
                nc.vector.tensor_tensor(f_b[:, :, :], f_bf[:, :, :],
                                        consts["ffn_bias"][:, :].unsqueeze(1).to_broadcast([P, C, D]), ALU.add)\
                    .then_inc(s["ffn_biased"], 1)
            if slot == 6 and live(i, -2):
                b = i - 2
                wait(dve, s["ffn_biased"], b + 1)
                norm_stats(nc, dve, lambda c: f_b[:, c, :], bn_d, mv_d, s["stat_d_raw"], s["stat_d"], C, b, past_wait)

        for p in range(NP):
            j, b = (p + 6) % NP, (i if p < 2 else i + 1)
            for c in range(C):
                if live(b, 0):
                    wait(dve, s["max_ps"], 32 * b + 4 * j + c + 1)
                    if j % 4 == 0 and c == 0:
                        wait(dve, s["max_split"], 4 * (2 * (b - 1) + j // 4 + 1))
                    nc.vector.tensor_reduce(neg_max[j // 4][:, c, j % 4, :], score_ps[c % 2][:, :, :], AX_X, ALU.max,
                                            negate=True).then_inc(s["max_read"], 1)
                if c % 2:
                    side(2 * p + c // 2)

    def per_token(x):
        return x.unsqueeze(2).to_broadcast([P, C, D])

    def pool(gp, i, par):
        if live(i, 1):
            b = i + 1
            wait_apart(gp, s["k_lo"], 2 * (b + 1), past_wait)
            wait_apart(gp, s["st_ready"], 64 * b - 64, past_wait)
            for r, part in enumerate(K_PART):
                gp.dma_start(k_stack[1 - par][64 + HD * r:64 + HD * (r + 1), :, :], k_parts[64:128, part, :])\
                    .then_inc(s["kstack_ready"], 16)
        TT, TS = nc.gpsimd.tensor_tensor, nc.gpsimd.tensor_scalar
        t = lambda n: tiny[:, n, :]
        half_neg, half = consts["pow"][:, 0, :], consts["pow"][:, 1, :]
        neg_one = consts["pow"][:, 2, :]

        def x_of(b):
            return x_all[:, b, :].rearrange("p (c d) -> p c d", c=C)

        if live(i, 2):
            b = i + 2
            q, at0 = s["prep_step"], 9 * b
            wait_apart(gp, s["stat_a"], C * (b + 1), past_wait)
            TS(t(0), mv_a[:, :, 1], EPS, None, ALU.add).then_inc(q, 1)
            nc.gpsimd.tensor_copy(mean_rs[:, b, 0, :], mv_a[:, :, 0]).then_inc(q, 1)
            wait_apart(gp, q, at0 + 1, past_wait)
            TT(mean_rs[:, b, 1, :], t(0), half_neg, ALU.pow).then_inc(q, 1)
            wait_apart(gp, q, at0 + 3, past_wait)
            TT(t(1), mv_a[:, :, 1], mean_rs[:, b, 1, :], ALU.mult).then_inc(q, 1)
            wait_apart(gp, q, at0 + 4, past_wait)
            TT(t(2), t(1), mean_rs[:, b, 1, :], ALU.mult).then_inc(q, 1)
            wait_apart(gp, q, at0 + 5, past_wait)
            TS(t(3), t(2), EPS, None, ALU.add).then_inc(q, 1)
            wait_apart(gp, q, at0 + 6, past_wait)
            TT(t(4), t(3), half_neg, ALU.pow).then_inc(q, 1)
            wait_apart(gp, q, at0 + 7, past_wait)
            TT(t(5), t(4), mean_rs[:, b, 1, :], ALU.mult).then_inc(q, 1)
            wait_apart(gp, s["y_step"], 4 * (b - 3), past_wait)
            TT(centred[:, :, :], x_of(b), per_token(mean_rs[:, b, 0, :]), ALU.subtract).then_inc(q, 1)
            wait_apart(gp, q, at0 + 9, past_wait)
            wait_apart(gp, s["znT_ps"], b, past_wait)
            TT(zn[:, :, :], centred[:, :, :], per_token(t(5)), ALU.mult).then_inc(s["zn_ready"], 1)
        if live(i, -1):
            b = i - 1
            q, at0 = s["zres_step"], 3 * b
            wait_apart(gp, s["att_ready"], b, past_wait)
            TT(z_res[:, :, :], x_of(b), per_token(mean_rs[:, b, 0, :]), ALU.subtract).then_inc(q, 1)
            wait_apart(gp, q, at0 + 1, past_wait)
            TT(z_res[:, :, :], z_res[:, :, :], per_token(mean_rs[:, b, 1, :]), ALU.mult).then_inc(q, 1)
            wait_apart(gp, q, at0 + 2, past_wait)
            TT(z_res[:, :, :], z_res[:, :, :], consts["b_proj"][:, :].unsqueeze(1).to_broadcast([P, C, D]),
               ALU.add).then_inc(q, 1)

        if live(i, -2):
            b = i - 2
            q, at0 = s["x2_step"], 10 * b
            wait_apart(gp, s["stat_d"], C * (b + 1), past_wait)
            nc.gpsimd.tensor_copy(tiny_bf[:, 0, :], mv_d[:, :, 0]).then_inc(q, 1)
            nc.gpsimd.tensor_copy(tiny_bf[:, 1, :], mv_d[:, :, 1]).then_inc(q, 1)
            wait_apart(gp, q, at0 + 2, past_wait)
            TT(f_c[:, :, :], f_b[:, :, :], per_token(tiny_bf[:, 0, :]), ALU.subtract).then_inc(q, 1)
            TS(tiny_bf[:, 2, :], tiny_bf[:, 1, :], EPS, None, ALU.add).then_inc(q, 1)
            wait_apart(gp, q, at0 + 4, past_wait)
            TT(tiny_bf[:, 3, :], tiny_bf[:, 2, :], half, ALU.pow).then_inc(q, 1)
            wait_apart(gp, q, at0 + 5, past_wait)
            TT(t(6), tiny_bf[:, 3, :], neg_one, ALU.pow).then_inc(q, 1)
            wait_apart(gp, q, at0 + 6, past_wait)
            TT(t(7), t(6), poison[:, :], ALU.add).then_inc(q, 1)
            wait_apart(gp, q, at0 + 7, past_wait)
            TT(f_c[:, :, :], f_c[:, :, :], per_token(t(7)), ALU.mult).then_inc(q, 1)
            wait_apart(gp, q, at0 + 8, past_wait)
            TT(x_of(b), x_of(b), f_c[:, :, :], ALU.add).then_inc(q, 2)
        def split(n, parts, rest):
            b = i + 2
            wait_apart(gp, s[n + "_r"], b + 1, past_wait)
            TS(parts[:, 1, :], rest[:, :], 1.0, None, ALU.mult).then_inc(s[n + "_lo"], 1)
            wait_apart(gp, s[n + "_lo"], 2 * b + 1, past_wait)
            TT(parts[:, 2, :], rest[:, :], parts[:, 1, :], ALU.subtract).then_inc(s[n + "_lo"], 1)

        if live(i, -1):
            b = i - 1
            q, at0 = s["x1_step"], 5 * b
            wait_apart(gp, s["stat_b"], C * (b + 1), past_wait)
            TS(t(0), mv_b[:, :, 1], EPS, None, ALU.add).then_inc(q, 1)
            wait_apart(gp, s["zn_ready"], min(b + 4, NB) if isinstance(b, int) else b + 4, past_wait)
            TT(att_c[:, :, :], att[:, :, :], per_token(mv_b[:, :, 0]), ALU.subtract).then_inc(q, 1)
            wait_apart(gp, q, at0 + 2, past_wait)
            TT(t(1), t(0), half_neg, ALU.pow).then_inc(q, 1)
            wait_apart(gp, q, at0 + 3, past_wait)
            TT(att_c[:, :, :], att_c[:, :, :], per_token(t(1)), ALU.mult).then_inc(q, 1)
            wait_apart(gp, q, at0 + 4, past_wait)
            TT(x_of(b), x_of(b), att_c[:, :, :], ALU.add).then_inc(q, 1)
        if live(i, 2):
            split("q", q_parts, q_rest)
        if live(i, -1):
            b = i - 1
            q, at0 = s["y_step"], 4 * b
            wait_apart(gp, s["stat_c"], C * (b + 1), past_wait)
            TS(t(0), mv_c[:, :, 1], EPS, None, ALU.add).then_inc(q, 1)
            TT(att_c[:, :, :], x_of(b), per_token(mv_c[:, :, 0]), ALU.subtract).then_inc(q, 1)
            wait_apart(gp, q, at0 + 2, past_wait)
            TT(t(1), t(0), half_neg, ALU.pow).then_inc(q, 1)
            wait_apart(gp, q, at0 + 3, past_wait)
            wait_apart(gp, s["quant_step"], 10 * b, past_wait)
            TT(y_bf[:, :, :], att_c[:, :, :], per_token(t(1)), ALU.mult).then_inc(q, 1)
        if live(i, 2):
            split("k", k_parts, k_rest)

    def sync(sp, i, par):
        if live(i, 2):
            wait_apart(sp, x_loaded, 16 * (i + 2), past_wait)
            sp.dma_start(x_all[:, i + 2, :].rearrange("p (c d) -> p c d", c=C),
                         x_in[i + 2].rearrange("(c p) d -> p c d", p=P)).then_inc(x_loaded, 16)
        if live(i, 1):
            b = i + 1
            wait_apart(sp, s["q_lo"], 2 * (b + 1), past_wait)
            wait_apart(sp, s["k_lo"], 2 * (b + 1), past_wait)
            wait_apart(sp, s["st_ready"], 64 * b - 64, past_wait)
            for parts, stack, order in ((q_parts, q_stack[1 - par], Q_PART), (k_parts, k_stack[1 - par], K_PART)):
                for h in range(1 if stack in k_stack else 2):
                    for r, part in enumerate(order):
                        sp.dma_start(stack[64 * h + HD * r:64 * h + HD * (r + 1), :, :],
                                     parts[64 * h:64 * h + 64, part, :]).then_inc(s["stack_ready"], 16)
        for half, off in ((1, 0), (0, 1)):
            if live(i, off):
                n = 2 * (i + off) + half
                wait_apart(sp, s["maxT_read"], n + 1, past_wait)
                wait_apart(sp, s["mrow_ready"], 16 * MROW_DMAS * n, past_wait)
                for h in range(2):
                    sp.dma_start(q_stack[par ^ off][64 * h + KROWS:64 * h + KROWS + MROWS, 4 * half:4 * half + 4, :],
                                 max_rows[12 * h:12 * h + 12, :])\
                        .then_inc(s["mrow_ready"], 16)

    def iterate(eng, step):
        for i in range(-2, 4):
            step(eng, i, i % 2)
        with eng.Fori(0, NB // 2 - 3) as two:
            step(eng, two * 2 + 4, 0)
            step(eng, two * 2 + 5, 1)
        for i in range(NB - 2, NB + 2):
            step(eng, i, i % 2)

    return {"tensor": tensor, "scalar": scalar, "vector": vector, "pool": pool, "sync": sync,
            "iterate": iterate, "stacks": (*q_stack, *k_stack), "v_pad": v_pad, "probs": probs, "zn": zn}


def hawk_moe_phase(nc, ctx, sems, psum, x_all, slots, padded, acc_y, w, consts, out, NB, T):
    C = T // P
    E = consts["rev"].shape[2]
    CAPACITY = 100
    TAPS = 4
    assert NB * C <= 256

    def sb(name, shape, dt=F32):
        return ctx.enter_context(nc.sbuf_tensor(name, shape, dt))

    two = lambda n: slots[:, n:n + 2, :]
    one = lambda n: slots[:, n, :]
    conv, gate_g = (two(0), two(2)), (two(4), two(6))
    tan_f, inp, alpha, beta, h, gh, grown = (two(n) for n in range(8, 22, 2))
    xn, z3, xh, xn2, t, h4, y, xT, xn2T, h4T = (one(n) for n in range(22, 32))
    xc_pad = padded[:, 0:2 * (T + TAPS - 1)].rearrange("p (n t) -> p n t", n=2)
    stats = {n: (sb(f"bn_{n}", [P, C, 6]), sb(f"mv_{n}", [P, C, 2])) for n in ("h", "t", "x3", "y")}
    stats["x2_0"], stats["x2_1"] = [(sb(f"bn_x2_{k}", [P, C, 6]), sb(f"mv_x2_{k}", [P, C, 2])) for k in range(2)]
    rs_x2 = [sb(f"rs_x2_{k}", [P, 3, C]) for k in range(2)]
    rs = {n: sb(f"rs_{n}", [P, 3, C]) for n in ("h", "t", "x3", "y")}
    top = sb("top", [P, 8, C])
    exps = sb("exps", [P, C, E])
    shifted = sb("shifted", [P, C, E])
    ranked = sb("ranked", [P, C, E])
    placed = sb("placed", [P, C, E])
    chosen = sb("chosen", [P, C, E], BF16)
    counts = sb("counts", [P, C + 1, E], BF16)

    pair0, pair1, bank_t, bank_o, bank_y, bank_r = psum
    log_ps = bank_r[:, 0:C * E]
    cum_ps = bank_r[:, 2 * C * E:3 * C * E]

    names = ("stat_x2_raw stat_x2 rs_x2_step xn_ready xT_ps xT_ready xc_ps xc_copied conv_init conv_step gate_ps gate_ready "
             "forget_ps tanf_ready alpha_ready sq_ready om_ready beta_ready inp_ps inp_tanh u_ready xs_ready h_ready "
             "gh_ready z3_ready wout_ps xh_ready stat_h_raw stat_h rs_h_step xn2_ready xn2T_ps xn2T_ready "
             "mg_ps mg_ready mx_ps grown_ready shrink_ps t_ready stat_t_raw stat_t rs_t_step tn_ready x3_ready "
             "stat_x3_raw stat_x3 rs_x3_step h4_ready h4T_ps h4T_ready y_ps y_ready stat_y_raw stat_y rs_y_step logits_ps "
             "top_step exps_ready route_step count_step cum_ready place_step yc_ready yn_ready x4_ready").split()
    s = {n: ctx.enter_context(nc.semaphore("l1_" + n)) for n in names}
    past_wait = sems["past_wait"]

    def live(i, off):
        return not isinstance(i, int) or 0 <= i + off < NB

    PAIR0 = [("forget", -1, s["tanf_ready"], 2, 2), ("inp", -1, s["inp_tanh"], 2, 2), ("gate", 0, s["gate_ready"], 1, 1)]
    PAIR1 = [("xc", 0, s["conv_init"], 2, 2), ("mg", -2, s["mg_ready"], 1, 1), ("mx", -2, s["grown_ready"], 1, 1)]
    BANK_T = [("xT", 0, s["xT_ready"], 1, 1), ("xn2T", -2, s["xn2T_ready"], 1, 1), ("h4T", -3, s["h4T_ready"], 1, 1)]
    BANK_O = [("wout", -2, s["xh_ready"], 1, 1), ("shrink", -2, s["t_ready"], 1, 1)]

    def tensor(pe, i, par):
        def b_of(off):
            return i + off

        def transpose4(src, done):
            for c in range(C):
                mm = nc.tensor.transpose(bank_t[:, c * P:(c + 1) * P], src[:, c * P:(c + 1) * P],
                                         consts["ident"][:, :])
            mm.then_inc(done, 1)

        def two_chunks(dst, weight, first, src, done):
            K = len(src)
            for n in range(2):
                for k in range(K):
                    mm = nc.tensor.matmul(dst[:, n, :], weight[:, k, (first + n) * P:(first + n + 1) * P], src[k],
                                          start=(k == 0), stop=(k == K - 1))
            mm.then_inc(done, 1)

        def natural(dst, src, weight, done):
            for c in range(C):
                for k in range(2):
                    mm = nc.tensor.matmul(dst[:, c * D:(c + 1) * D], src[:, k, c * P:(c + 1) * P], weight[:, k, :],
                                          start=(k == 0), stop=(k == 1))
            mm.then_inc(done, 1)

        conv_par = conv[(par + 1) & 1]
        if live(i, -2):
            b = b_of(-2)
            wait(pe, s["gh_ready"], b + 1)
            bank_free(pe, i, live, BANK_O, "wout")
            natural(bank_o, gh, w["out"], s["wout_ps"])
        if live(i, 0):
            wait(pe, s["xn_ready"], C * (i + 1))
            bank_free(pe, i, live, BANK_T, "xT")
            transpose4(xn, s["xT_ps"])
        if live(i, -1):
            b = b_of(-1)
            wait(pe, s["conv_step"], 2 * (TAPS - 1) * (b + 1))
            bank_free(pe, i, live, PAIR0, "forget")
            two_chunks(pair0, w["gates"], 0, [conv_par[:, k, :] for k in range(2)], s["forget_ps"])
        if live(i, 0):
            wait(pe, s["xT_ready"], i + 1)
            bank_free(pe, i, live, PAIR1, "xc")
            two_chunks(pair1, w["in"], 2, [xT], s["xc_ps"])
        if live(i, -2):
            b = b_of(-2)
            wait(pe, s["xn2_ready"], b + 1)
            bank_free(pe, i, live, BANK_T, "xn2T")
            transpose4(xn2, s["xn2T_ps"])
        if live(i, -1):
            bank_free(pe, i, live, PAIR0, "inp")
            two_chunks(pair0, w["gates"], 2, [conv_par[:, k, :] for k in range(2)], s["inp_ps"])
        if live(i, -4):
            b = b_of(-4)
            wait(pe, s["count_step"], (C + 1) * (b + 1))
            wait(pe, s["place_step"], 3 * b)
            nc.tensor.matmul(cum_ps, consts["tri"][:, :], chosen[:, :, :].rearrange("p c e -> p (c e)"),
                             start=True, stop=False)
            nc.tensor.matmul(cum_ps, consts["ones"][:, :], counts[:, 0:C, :].rearrange("p c e -> p (c e)"),
                             start=False, stop=True).then_inc(s["cum_ready"], 1)
        if live(i, -2):
            b = b_of(-2)
            wait(pe, s["xn2T_ready"], b + 1)
            bank_free(pe, i, live, PAIR1, "mg")
            two_chunks(pair1, w["grow"], 0, [xn2T], s["mg_ps"])
        if live(i, 0):
            bank_free(pe, i, live, PAIR0, "gate")
            two_chunks(pair0, w["in"], 0, [xT], s["gate_ps"])
        if live(i, -3):
            b = b_of(-3)
            wait(pe, s["h4_ready"], C * (b + 1))
            bank_free(pe, i, live, BANK_T, "h4T")
            transpose4(h4, s["h4T_ps"])
        if live(i, -2):
            bank_free(pe, i, live, PAIR1, "mx")
            two_chunks(pair1, w["grow"], 2, [xn2T], s["mx_ps"])
        if live(i, -3):
            b = b_of(-3)
            wait(pe, s["h4T_ready"], b + 1)
            wait(pe, s["y_ready"], b)
            wait(pe, s["top_step"], 2 * b)
            wait(pe, s["place_step"], 3 * b - 2)
            for c in range(C):
                mm = nc.tensor.matmul(log_ps[:, c * E:(c + 1) * E], h4T[:, c * P:(c + 1) * P], w["route"][:, :],
                                      start=True, stop=True)
            mm.then_inc(s["logits_ps"], 1)
            for c in range(C):
                mm = nc.tensor.matmul(bank_y[:, c * D:(c + 1) * D], h4T[:, c * P:(c + 1) * P], w["expert"][:, :],
                                      start=True, stop=True)
            mm.then_inc(s["y_ps"], 1)
        if live(i, -2):
            b = b_of(-2)
            wait(pe, s["grown_ready"], b + 1)
            bank_free(pe, i, live, BANK_O, "shrink")
            natural(bank_o, grown, w["shrink"], s["shrink_ps"])

    def scalar(act, i, par):
        A = nc.scalar.activation
        if live(i, -4):
            b = i - 4
            wait(act, s["top_step"], 2 * (b + 1))
            wait(act, s["route_step"], 8 * b)
            A(exps[:, :, :], shifted[:, :, :], ACT.Exp).then_inc(s["exps_ready"], 1)
        if live(i, -1):
            b = i - 1
            wait(act, s["forget_ps"], b + 1)
            wait(act, s["alpha_ready"], 2 * b)
            for n in range(2):
                A(tan_f[:, n, :], pair0[:, n, :], ACT.Tanh, bias=consts["b_half"][:, n:n + 1], scale=0.5)\
                    .then_inc(s["tanf_ready"], 1)
            wait(act, s["h_ready"], 2 * b)
            wait(act, s["sq_ready"], b)
            for n in range(2):
                wait(act, s["tanf_ready"], 2 * b + n + 1)
                A(alpha[:, n, :], tan_f[:, n, :], ACT.Exp, bias=consts["k_half"][:, n:n + 1],
                  scale=consts["k_half"][:, n:n + 1]).then_inc(s["alpha_ready"], 1)
            wait(act, s["alpha_ready"], 2 * (b + 1))
            wait(act, s["xs_ready"], b)
            A(beta, alpha, ACT.Square).then_inc(s["sq_ready"], 1)
        if live(i, 0):
            wait(act, s["xT_ps"], i + 1)
            wait(act, s["gate_ps"], i)
            A(xT, bank_t[:, :], ACT.Copy, scale=consts["gamma1"][:, 0:1]).then_inc(s["xT_ready"], 1)
            wait(act, s["xc_ps"], i + 1)
            wait(act, s["conv_step"], 2 * (TAPS - 1) * i)
            A(xc_pad[:, :, TAPS - 1:], pair1[:, :, :], ACT.Copy).then_inc(s["xc_copied"], 1)
            wait(act, s["inp_ps"], i - 1)
            wait(act, s["u_ready"], i - 1)
            for n in range(2):
                A(conv[par][:, n, :], pair1[:, n, :], ACT.Identity, bias=consts["conv_b"][:, n:n + 1],
                  scale=consts["conv_w"][:, n, TAPS - 1:TAPS]).then_inc(s["conv_init"], 1)
        if live(i, -2):
            b = i - 2
            wait(act, s["xn2T_ps"], b + 1)
            wait(act, s["mx_ps"], b)
            A(xn2T, bank_t[:, :], ACT.Copy, scale=consts["gamma2"][:, 0:1]).then_inc(s["xn2T_ready"], 1)
        if live(i, -1):
            b = i - 1
            wait(act, s["om_ready"], b + 1)
            A(beta, beta, ACT.Sqrt, bias=consts["tiny"][:, 0:1]).then_inc(s["beta_ready"], 1)
            wait(act, s["inp_ps"], b + 1)
            wait(act, s["h_ready"], 2 * b)
            for n in range(2):
                A(inp[:, n, :], pair0[:, n, :], ACT.Tanh, bias=consts["b_half"][:, 2 + n:3 + n], scale=0.5)\
                    .then_inc(s["inp_tanh"], 1)
        if live(i, -2):
            b = i - 2
            wait(act, s["mg_ps"], b + 1)
            wait(act, s["shrink_ps"], b)
            A(grown, pair1[:, :, :], ACT.Gelu).then_inc(s["mg_ready"], 1)
        if live(i, 0):
            wait(act, s["gate_ps"], i + 1)
            wait(act, s["gh_ready"], i - 1)
            A(gate_g[par], pair0[:, :, :], ACT.Gelu).then_inc(s["gate_ready"], 1)
        if live(i, -3):
            b = i - 3
            wait(act, s["h4T_ps"], b + 1)
            wait(act, s["y_ps"], b)
            A(h4T, bank_t[:, :], ACT.Copy).then_inc(s["h4T_ready"], 1)

    def vector(dve, i, par):
        TT, TS, STT = nc.vector.tensor_tensor, nc.vector.tensor_scalar, nc.vector.scalar_tensor_tensor

        def bn(which, name, src, b):
            raw, mv = stats[which]
            norm_stats(nc, dve, src, raw, mv, s[f"stat_{name}_raw"], s[f"stat_{name}"], C, b, past_wait)

        def scaled(dst, src, mv, r, done):
            for c in range(C):
                TS(dst[:, c * D:(c + 1) * D], src(c), mv[:, c, 0:1], r[:, c:c + 1], ALU.subtract, ALU.mult)\
                    .then_inc(done, 1)

        chunk = lambda x: (lambda c: x[:, c * D:(c + 1) * D])
        if live(i, -3):
            b = i - 3
            wait(dve, s["shrink_ps"], b + 1)
            wait(dve, s["tn_ready"], C * b)
            wait(dve, s["x3_ready"], b)
            TT(t, xh, bank_o[:, :], ALU.add).then_inc(s["t_ready"], 1)
            wait(dve, s["t_ready"], b + 1)
            wait(dve, s["tn_ready"], C * b)
            bn("t", "t", chunk(t), b)
        if live(i, -4):
            b = i - 4
            q = s["top_step"]
            wait(dve, s["logits_ps"], b + 1)
            nc.vector.tensor_reduce(top[:, 0, :], log_ps.rearrange("p (c e) -> p c e", e=E), AX_X, ALU.max)\
                .then_inc(q, 1)
            wait(dve, q, 2 * b + 1)
            wait(dve, s["route_step"], 8 * b)
            wait(dve, s["exps_ready"], b)
            TT(shifted[:, :, :], log_ps.rearrange("p (c e) -> p c e", e=E),
               top[:, 0, :].unsqueeze(2).to_broadcast([P, C, E]), ALU.subtract).then_inc(q, 1)
            wait(dve, s["y_ps"], b + 1)
            wait(dve, s["yc_ready"], b)
            TT(y.rearrange("p (c d) -> p c d", c=C), bank_y[:, :].rearrange("p (c d) -> p c d", c=C),
               consts["b_expert"][:, :].unsqueeze(1).to_broadcast([P, C, D]), ALU.add).then_inc(s["y_ready"], 1)
        if live(i, -2):
            b = i - 2
            wait(dve, s["wout_ps"], b + 1)
            wait(dve, s["z3_ready"], C * (b + 1))
            wait(dve, s["xn2_ready"], b)
            wait(dve, s["t_ready"], b)
            TT(xh, z3, bank_o[:, :], ALU.add).then_inc(s["xh_ready"], 1)
            wait(dve, s["xh_ready"], b + 1)
            wait(dve, s["rs_h_step"], 3 * b)
            bn("h", "h", chunk(xh), b)
        if live(i, -4):
            b = i - 4
            wait(dve, s["y_ready"], b + 1)
            wait(dve, s["yc_ready"], b)
            bn("y", "y", chunk(y), b)
        if live(i, -3):
            b = i - 3
            wait(dve, s["rs_t_step"], 2 * (b + 1))
            scaled(t, chunk(t), stats["t"][1], rs["t"][:, 1, :], s["tn_ready"])
        if live(i, -4):
            b = i - 4
            q, at = s["route_step"], 8 * b
            wait(dve, s["top_step"], 2 * (b + 1))
            STT(ranked[:, :, :], shifted[:, :, :], 0.0, consts["rev"][:, :, :], ALU.is_ge, ALU.mult).then_inc(q, 1)
            wait(dve, q, at + 1)
            nc.vector.tensor_reduce(top[:, 1, :], ranked[:, :, :], AX_X, ALU.max).then_inc(q, 1)
            wait(dve, q, at + 2)
            wait(dve, s["cum_ready"], b)
            wait(dve, s["place_step"], 3 * b)
            TT(chosen[:, :, :], consts["rev"][:, :, :], top[:, 1, :].unsqueeze(2).to_broadcast([P, C, E]),
               ALU.is_equal).then_inc(q, 1)
            wait(dve, s["exps_ready"], b + 1)
            nc.vector.tensor_reduce(top[:, 2, :], exps[:, :, :], AX_X, ALU.add).then_inc(q, 1)
            wait(dve, q, at + 4)
            nc.vector.reciprocal(top[:, 3, :], top[:, 2, :]).then_inc(q, 1)
            wait(dve, q, at + 5)
            TT(top[:, 4, :], top[:, 3, :], top[:, 3, :], ALU.mult).then_inc(q, 1)
            wait(dve, q, at + 6)
            wait(dve, s["stat_y"], C * (b + 1))
            TT(top[:, 5, :], top[:, 4, :], stats["y"][1][:, :, 1], ALU.mult).then_inc(q, 1)
            wait(dve, q, at + 7)
            wait(dve, s["rs_y_step"], 2 * b)
            TS(rs["y"][:, 0, :], top[:, 5, :], EPS, None, ALU.add).then_inc(q, 1)
            q, at = s["count_step"], (C + 1) * b
            wait(dve, q, at)
            nc.vector.tensor_copy(counts[:, 0, :], counts[:, C, :]).then_inc(q, 1)
            for c in range(C):
                wait(dve, q, at + 1 + c)
                TT(counts[:, c + 1, :], counts[:, c, :], chosen[:, c, :], ALU.add).then_inc(q, 1)
        if live(i, -3):
            b = i - 3
            wait(dve, s["x3_ready"], b + 1)
            wait(dve, s["h4_ready"], C * b)
            bn("x3", "x3", lambda c: x_all[:, b, c * D:(c + 1) * D], b)
        if live(i, 0):
            q, at = s["conv_step"], 2 * (TAPS - 1) * i
            for tap in range(TAPS - 1):
                if tap == 0:
                    wait(dve, s["xc_copied"], i + 1)
                    wait(dve, s["conv_init"], 2 * (i + 1))
                else:
                    wait(dve, q, at + 2 * tap)
                for n in range(2):
                    STT(conv[par][:, n, :], xc_pad[:, n, tap:tap + T], consts["conv_w"][:, n, tap:tap + 1],
                        conv[par][:, n, :], ALU.mult, ALU.add).then_inc(q, 1)
        if live(i, -1):
            b = i - 1
            cv = conv[(par + 1) & 1]
            wait(dve, s["inp_tanh"], 2 * (b + 1))
            STT(inp, inp, 1.0, cv, ALU.add, ALU.mult).then_inc(s["u_ready"], 1)
        if live(i, -3):
            b = i - 3
            wait(dve, s["rs_x3_step"], 2 * (b + 1))
            wait(dve, s["h4T_ps"], b)
            scaled(h4, lambda c: x_all[:, b, c * D:(c + 1) * D], stats["x3"][1], rs["x3"][:, 1, :], s["h4_ready"])
        if live(i, -4):
            b = i - 4
            q, at = s["place_step"], 3 * b
            wait(dve, s["cum_ready"], b + 1)
            TT(placed[:, :, :], chosen[:, :, :], cum_ps.rearrange("p (c e) -> p c e", e=E), ALU.mult).then_inc(q, 1)
            wait(dve, q, at + 1)
            nc.vector.tensor_reduce(top[:, 6, :], placed[:, :, :], AX_X, ALU.add).then_inc(q, 1)
            wait(dve, q, at + 2)
            wait(dve, s["rs_y_step"], 2 * b)
            STT(top[:, 7, :], top[:, 6, :], float(CAPACITY), top[:, 3, :], ALU.is_le, ALU.mult).then_inc(q, 1)
        if live(i, -1):
            b = i - 1
            wait(dve, s["u_ready"], b + 1)
            wait(dve, s["beta_ready"], b + 1)
            STT(inp, inp, 0.5, beta, ALU.mult, ALU.mult).then_inc(s["xs_ready"], 1)
            wait(dve, s["xs_ready"], b + 1)
            wait(dve, s["gh_ready"], b)
            for n in range(2):
                nc.vector.tensor_tensor_scan(h[:, n, :], alpha[:, n, :], inp[:, n, :], 0.0, ALU.mult, ALU.add)\
                    .then_inc(s["h_ready"], 1)
        if live(i, -2):
            b = i - 2
            wait(dve, s["mx_ps"], b + 1)
            wait(dve, s["mg_ready"], b + 1)
            TT(grown, grown, pair1[:, :, :], ALU.mult).then_inc(s["grown_ready"], 1)
        if live(i, -1):
            b = i - 1
            p = (par + 1) & 1
            wait(dve, s["xh_ready"], b)
            scaled(z3, lambda c: x_all[:, b, c * D:(c + 1) * D], stats[f"x2_{p}"][1], rs_x2[p][:, 1, :],
                   s["z3_ready"])
        if live(i, 1):
            b = i + 1
            p = (par + 1) & 1
            wait(dve, sems["x2_step"], 10 * (b + 1))
            wait(dve, s["z3_ready"], C * (b - 1))
            bn(f"x2_{p}", "x2", lambda c: x_all[:, b, c * D:(c + 1) * D], b)
            wait(dve, s["rs_x2_step"], 3 * (b + 1))
            wait(dve, s["xT_ps"], b)
            scaled(xn, lambda c: x_all[:, b, c * D:(c + 1) * D], stats[f"x2_{p}"][1], rs_x2[p][:, 2, :],
                   s["xn_ready"])

    def pool(gp, i, par):
        TT, TS = nc.gpsimd.tensor_tensor, nc.gpsimd.tensor_scalar
        half_neg = consts["pow"][:, 0, :]
        per_token = lambda x: x.unsqueeze(2).to_broadcast([P, C, D])
        rows = lambda x: x.rearrange("p (c d) -> p c d", c=C)

        def rsqrt(name, b):
            q, mv, r = s[f"rs_{name}_step"], stats[name][1], rs[name]
            wait_apart(gp, s[f"stat_{name}"], C * (b + 1), past_wait)
            TS(r[:, 0, :], mv[:, :, 1], EPS, None, ALU.add).then_inc(q, 1)
            wait_apart(gp, q, 2 * b + 1, past_wait)
            TT(r[:, 1, :], r[:, 0, :], half_neg, ALU.pow).then_inc(q, 1)

        if live(i, -3):
            rsqrt("t", i - 3)
        if live(i, -2):
            b = i - 2
            q, mv, r = s["rs_h_step"], stats["h"][1], rs["h"]
            wait_apart(gp, s["stat_h"], C * (b + 1), past_wait)
            TT(r[:, 0, :], mv[:, :, 0], mv[:, :, 0], ALU.mult).then_inc(q, 1)
            wait_apart(gp, q, 3 * b + 1, past_wait)
            TT(r[:, 1, :], r[:, 0, :], mv[:, :, 1], ALU.add).then_inc(q, 1)
            wait_apart(gp, q, 3 * b + 2, past_wait)
            TT(r[:, 2, :], r[:, 1, :], half_neg, ALU.pow).then_inc(q, 1)
            wait_apart(gp, q, 3 * b + 3, past_wait)
            wait_apart(gp, s["xn2T_ps"], b, past_wait)
            TT(rows(xn2), rows(xh), per_token(r[:, 2, :]), ALU.mult).then_inc(s["xn2_ready"], 1)
        if live(i, -3):
            b = i - 3
            wait_apart(gp, s["tn_ready"], C * (b + 1), past_wait)
            TT(x_all[:, b, :], x_all[:, b, :], t, ALU.add).then_inc(s["x3_ready"], 1)
        if live(i, -1):
            b = i - 1
            wait_apart(gp, s["sq_ready"], b + 1, past_wait)
            TS(beta, beta, -1.0, 1.0, ALU.mult, ALU.add).then_inc(s["om_ready"], 1)
        if live(i, -3):
            rsqrt("x3", i - 3)
        if live(i, -4):
            b = i - 4
            wait_apart(gp, s["route_step"], 8 * (b + 1), past_wait)
            TT(rs["y"][:, 1, :], rs["y"][:, 0, :], half_neg, ALU.pow).then_inc(s["rs_y_step"], 1)
            wait_apart(gp, s["x4_ready"], b, past_wait)
            TT(rows(acc_y), rows(y), per_token(stats["y"][1][:, :, 0]), ALU.subtract).then_inc(s["yc_ready"], 1)
        if live(i, 1):
            b = i + 1
            p = (par + 1) & 1
            q, mv, r = s["rs_x2_step"], stats[f"x2_{p}"][1], rs_x2[p]
            wait_apart(gp, s["stat_x2"], C * (b + 1), past_wait)
            TT(r[:, 2, :], mv[:, :, 1], half_neg, ALU.pow).then_inc(q, 1)
            TS(r[:, 0, :], mv[:, :, 1], EPS, None, ALU.add).then_inc(q, 1)
            wait_apart(gp, q, 3 * b + 2, past_wait)
            TT(r[:, 1, :], r[:, 0, :], half_neg, ALU.pow).then_inc(q, 1)
        if live(i, -1):
            b = i - 1
            wait_apart(gp, s["h_ready"], 2 * (b + 1), past_wait)
            wait_apart(gp, s["gate_ready"], b + 1, past_wait)
            wait_apart(gp, s["wout_ps"], b, past_wait)
            TT(gh, h, gate_g[(par + 1) & 1], ALU.mult).then_inc(s["gh_ready"], 1)
        if live(i, -4):
            b = i - 4
            wait_apart(gp, s["place_step"], 3 * (b + 1), past_wait)
            wait_apart(gp, s["rs_y_step"], 2 * b + 1, past_wait)
            TT(rs["y"][:, 2, :], rs["y"][:, 1, :], top[:, 7, :], ALU.mult).then_inc(s["rs_y_step"], 1)
            wait_apart(gp, s["yc_ready"], b + 1, past_wait)
            wait_apart(gp, s["rs_y_step"], 2 * (b + 1), past_wait)
            TT(rows(acc_y), rows(acc_y), per_token(rs["y"][:, 2, :]), ALU.mult).then_inc(s["yn_ready"], 1)
            wait_apart(gp, s["yn_ready"], b + 1, past_wait)
            TT(x_all[:, b, :], x_all[:, b, :], acc_y, ALU.add).then_inc(s["x4_ready"], 1)

    def first(eng, name):
        wait(eng, sems["pv_done"], 16 * NB)
        if name == "tensor":
            wait(eng, sems["max_read"], 32 * NB)
            wait(eng, sems["exp_done"], 64 * NB)
            wait(eng, sems["acc_read"], 2 * NB)
            wait(eng, sems["ffn_read"], NB)

    def iterate(eng, step):
        for i in range(-1, 6):
            step(eng, i, i % 2)
        with eng.Fori(0, (NB - 8) // 2) as k:
            step(eng, k * 2 + 6, 0)
            step(eng, k * 2 + 7, 1)
        for i in range(NB - 2, NB + 4):
            step(eng, i, i % 2)

    def store(sp, stored):
        with sp.Fori(0, NB) as b:
            wait_apart(sp, s["x4_ready"], b + 1, past_wait)
            sp.dma_start(out[b].rearrange("(c p) d -> p c d", p=P),
                         x_all[:, b, :].rearrange("p (c d) -> p c d", c=C)).then_inc(stored, 16)
        sp.wait_ge(stored, 16 * NB)

    return {"tensor": tensor, "scalar": scalar, "vector": vector, "pool": pool, "store": store,
            "first": first, "iterate": iterate, "counts": counts, "xc_pad": xc_pad}


def build(nc, a, out):
    x_in = a["z"]
    NB, T = x_in.shape[0], x_in.shape[1]
    C = T // P
    E = a["w_gate"].shape[1]

    with ExitStack() as ctx:
        def sb(name, shape, dt=F32):
            return ctx.enter_context(nc.sbuf_tensor(name, shape, dt))

        def sem(name):
            return ctx.enter_context(nc.semaphore(name))

        psum = [ctx.enter_context(nc.psum_tensor(f"bank_pair{i}", [P, 2, T], F32)) for i in range(2)]
        psum += [ctx.enter_context(nc.psum_tensor(f"bank{i}", [P, T], F32)) for i in range(4)]
        x_all = sb("x_all", [P, NB, C * D])
        w = {"q": sb("w_q", [P, P]), "k": sb("w_k", [P, P]), "v": sb("w_v", [P, P]), "proj": sb("w_proj", [P, P]),
             "ffn": sb("w_ffn", [P, P], BF16)}
        w.update({"in": sb("w_in", [P, 1, 4 * P]), "gates": sb("w_gates", [P, 2, 4 * P]), "out": sb("w_out", [P, 2, P]),
                  "grow": sb("w_grow", [P, 1, 4 * P]), "shrink": sb("w_shrink", [P, 2, P]),
                  "route": sb("w_route", [P, E]), "expert": sb("w_expert", [P, P])})
        consts = {"ident": sb("ident", [P, P]), "ident_bf": sb("ident_bf", [P, P], BF16),
                  "pow": sb("pow", [P, 3, C]), "b_proj": sb("b_proj", [P, D]), "ffn_bias": sb("ffn_bias", [P, D], BF16),
                  "ln_scale": sb("ln_scale", [P, 1]), "ln_bias": sb("ln_bias", [P, 1]),
                  "s_in": sb("s_in", [P, 1]), "s_k": sb("s_k", [P, 1]), "s_in_inv": sb("s_in_inv", [P, 1]),
                  "s_k_inv": sb("s_k_inv", [P, 1]), "s_both": sb("s_both", [P, 1])}
        consts.update({"tri": sb("tri", [P, P], BF16), "ones": sb("ones", [P, P], BF16), "rev": sb("rev", [P, C, E]),
                       "conv_w": sb("conv_w", [P, 2, 4]), "conv_b": sb("conv_b", [P, 2]), "b_half": sb("b_half", [P, 4]),
                       "k_half": sb("k_half", [P, 2]), "gamma1": sb("gamma1", [P, 1]), "gamma2": sb("gamma2", [P, 1]),
                       "b_expert": sb("b_expert", [P, D]), "tiny": sb("tiny_c", [P, 1])})
        tri_raw = sb("tri_raw", [P, P])
        b_gates = sb("b_gates", [P, 4])
        soft = sb("soft", [P, 8, 2])
        ffn_raw = sb("ffn_raw", [P, D], BF16)
        loaded, pool_set, dve_set, dve_const = sem("loaded"), sem("pool_set"), sem("dve_set"), sem("dve_const")
        out_done = sem("out_done")
        sems = {"x_loaded": sem("x_loaded"), "past_wait": sem("past_wait")}
        att = attention_phase(nc, ctx, sems, psum, x_in, x_all, w, consts, NB)

        layer1 = hawk_moe_phase(nc, ctx, sems, psum, x_all, att["probs"],
                                att["v_pad"][1][:, :, :, :].rearrange("p c h e -> p (c h e)"),
                                att["zn"][:, :, :].rearrange("p c d -> p (c d)"), w, consts, out, NB, T)
        soft_step, loaded1, pool_set1 = sem("soft_step"), sem("loaded1"), sem("pool_set1")

        ffn_scaled, ffn_grid, ffn_under, ffn_over = (att["probs"][:, n, 0:D] for n in range(4))

        loads = [(w[n][:, :], a["w_" + n]) for n in ("q", "k", "v", "proj")]
        loads += [(ffn_raw[:, :], a["ffn_kernel"])]
        loads += [(consts[n][:, :], a[n].rearrange("(p a) -> p a", a=1)) for n in ("ln_scale", "ln_bias")]
        loads += [(consts[n][:, :], a[n].rearrange("(a d) -> a d", a=1).to_broadcast([P, a[n].shape[0]]))
                  for n in ("b_proj", "ffn_bias", "s_in", "s_k")]
        loads1 = [(w["in"][:, 0, :], a["w_in"]), (w["gates"][:, :, :], a["w_gates"].rearrange("(k p) n -> p k n", p=P)),
                  (w["out"][:, :, :], a["w_out"].rearrange("(k p) n -> p k n", p=P)), (w["grow"][:, 0, :], a["w_grow"]),
                  (w["shrink"][:, :, :], a["w_shrink"].rearrange("(k p) n -> p k n", p=P)),
                  (w["route"][:, :], a["w_gate"]), (w["expert"][:, :], a["w_expert"]),
                  (consts["conv_w"][:, :, :], a["conv_w"]), (consts["conv_b"][:, :], a["conv_b"]),
                  (b_gates[:, :], a["b_gates"]), (soft[:, 0, :], a["forget_base"]),
                  (consts["b_expert"][:, :], a["b_expert"].rearrange("(a d) -> a d", a=1).to_broadcast([P, D]))]
        loads1 += [(consts[n][:, :], a[n].rearrange("(p a) -> p a", a=1)) for n in ("gamma1", "gamma2")]
        LOADED1, POOL_SET1 = 16 * len(loads1), 5 + E
        TERMS = 8
        SOFT = 8 + TERMS
        LOADED, POOL_SET, DVE_SET = 16 * len(loads), 8, 10

        block = ctx.enter_context(nc.Block())

        @block.sync
        def _(sp):
            for dst, src in loads:
                sp.dma_start(dst, src).then_inc(loaded, 16)
            for dst, src in loads1:
                sp.dma_start(dst, src).then_inc(loaded1, 16)
            sp.wait_ge(pool_set, POOL_SET)
            att["iterate"](sp, att["sync"])
            layer1["store"](sp, out_done)

        @block.gpsimd
        def _(gp):
            ident, vs = consts["ident"], att["v_pad"]
            nc.gpsimd.memset(ident[:, :], 0.0).then_inc(pool_set, 1)
            for stack in att["stacks"]:
                nc.gpsimd.memset(stack[:, :, :], 1.0)
            for n, v in enumerate((-0.5, 0.5, -1.0)):
                nc.gpsimd.memset(consts["pow"][:, n, :], v).then_inc(pool_set, 1)
            for v in vs:
                nc.gpsimd.memset(v[:, :, :, :], 0.0).then_inc(pool_set, 1)
            gp.wait_ge(pool_set, 6)
            for n, v in enumerate(vs):
                dst = v[:, :, :, :].rearrange("p c (u t g) e -> p (c u) t g e", u=2, t=2)
                for t in range(2):
                    last = nc.gpsimd.memset(dst[:, :, t, :, 16 * t + 8:16 * t + 9], 1.0)
            last.then_inc(pool_set, 1)
            nc.gpsimd.affine_select(out=ident[:, :], in_=ident[:, :], compare_op=ALU.not_equal, fill=1.0, base=0,
                                    pattern=[[-1, P]], channel_multiplier=1).then_inc(pool_set, 1)
            gp.wait_ge(dve_set, DVE_SET)
            gp.wait_ge(pool_set, POOL_SET)
            nc.gpsimd.memset(tri_raw[:, :], 1.0).then_inc(pool_set1, 1)
            gp.wait_ge(pool_set1, 1)
            nc.gpsimd.affine_select(out=tri_raw[:, :], in_=tri_raw[:, :], compare_op=ALU.is_ge, fill=0.0, base=0,
                                    pattern=[[1, P]], channel_multiplier=-1).then_inc(pool_set1, 1)
            nc.gpsimd.memset(consts["ones"][:, :], 1.0).then_inc(pool_set1, 1)
            nc.gpsimd.memset(consts["tiny"][:, :], 1e-6).then_inc(pool_set1, 1)
            nc.gpsimd.memset(layer1["counts"][:, C, :], 0.0).then_inc(pool_set1, 1)
            for e in range(E):
                nc.gpsimd.memset(consts["rev"][:, :, e:e + 1], float(E - e)).then_inc(pool_set1, 1)
            att["iterate"](gp, att["pool"])
            layer1["first"](gp, "pool")
            nc.gpsimd.memset(layer1["xc_pad"][:, :, 0:3], 0.0).then_inc(pool_set1, 1)
            layer1["iterate"](gp, layer1["pool"])

        @block.vector
        def _(dve):
            TS = nc.vector.tensor_scalar
            dve.wait_ge(loaded, LOADED)
            nc.vector.reciprocal(consts["s_in_inv"][:, :], consts["s_in"][:, :]).then_inc(dve_set, 1)
            nc.vector.reciprocal(consts["s_k_inv"][:, :], consts["s_k"][:, :]).then_inc(dve_set, 1)
            nc.vector.tensor_tensor(consts["s_both"][:, :], consts["s_in"][:, :], consts["s_k"][:, :], ALU.mult)\
                .then_inc(dve_set, 1)
            dve.wait_ge(pool_set, POOL_SET)
            nc.vector.tensor_copy(consts["ident_bf"][:, :], consts["ident"][:, :]).then_inc(dve_set, 1)
            dve.wait_ge(dve_set, 2)
            TS(ffn_scaled, ffn_raw[:, :], consts["s_k_inv"][:, 0:1], None, ALU.mult).then_inc(dve_set, 1)
            dve.wait_ge(dve_set, 5)
            TS(ffn_grid.bitcast(U32), ffn_scaled.bitcast(U32), 0x7F800000, None, ALU.bitwise_and)\
                .then_inc(dve_set, 1)
            TS(ffn_over, ffn_scaled, 464.0, 464.0, ALU.max, ALU.subtract).then_inc(dve_const, 1)
            TS(ffn_under, ffn_scaled, -464.0, 464.0, ALU.min, ALU.add).then_inc(dve_const, 1)
            dve.wait_ge(dve_const, 2)
            nc.vector.tensor_tensor(ffn_over, ffn_over, ffn_under, ALU.subtract)\
                .then_inc(dve_const, 1)
            dve.wait_ge(dve_const, 3)
            TS(ffn_over, ffn_over, 1e30, 1e30, ALU.mult, ALU.mult).then_inc(dve_const, 1)
            dve.wait_ge(dve_const, 4)
            TS(ffn_over, ffn_over, 1e30, None, ALU.mult).then_inc(dve_const, 1)
            dve.wait_ge(dve_set, 6)
            TS(ffn_grid, ffn_grid, 2.0 ** -6, 1.5 * 2.0 ** 20, ALU.max, ALU.mult).then_inc(dve_set, 1)
            dve.wait_ge(dve_set, 7)
            nc.vector.tensor_tensor(ffn_scaled, ffn_scaled, ffn_grid, ALU.add).then_inc(dve_set, 1)
            dve.wait_ge(dve_set, 8)
            nc.vector.tensor_tensor(ffn_scaled, ffn_scaled, ffn_grid, ALU.subtract)\
                .then_inc(dve_set, 1)
            dve.wait_ge(dve_set, 9)
            dve.wait_ge(dve_const, 5)
            nc.vector.tensor_tensor(w["ffn"][:, :], ffn_scaled, ffn_over, ALU.add).then_inc(dve_set, 1)
            dve.wait_ge(dve_set, DVE_SET)
            att["iterate"](dve, att["vector"])
            q = soft_step
            dve.wait_ge(loaded1, LOADED1)
            dve.wait_ge(pool_set1, POOL_SET1)
            row = lambda n: soft[:, n, :]
            TS(row(1), row(0), -1.0, None, ALU.mult).then_inc(q, 1)
            dve.wait_ge(q, 1)
            nc.vector.tensor_tensor(row(1), row(0), row(1), ALU.max).then_inc(q, 1)
            TS(row(6), row(0), 0.0, -4.0, ALU.max, ALU.mult).then_inc(q, 1)
            dve.wait_ge(q, 4)
            TS(row(3), row(2), 2.0, None, ALU.add).then_inc(q, 1)
            dve.wait_ge(q, 5)
            nc.vector.reciprocal(row(3), row(3)).then_inc(q, 1)
            dve.wait_ge(q, 6)
            nc.vector.tensor_tensor(row(3), row(2), row(3), ALU.mult).then_inc(q, 1)
            dve.wait_ge(q, 7)
            nc.vector.tensor_tensor(row(4), row(3), row(3), ALU.mult).then_inc(q, 1)
            dve.wait_ge(q, 8)
            TS(row(5), row(4), 1.0 / (2 * TERMS - 1), None, ALU.mult).then_inc(q, 1)
            for n in range(TERMS - 2, 0, -1):
                dve.wait_ge(q, 7 + TERMS - n)
                nc.vector.scalar_tensor_tensor(row(5), row(5), 1.0 / (2 * n + 1), row(4), ALU.add, ALU.mult)\
                    .then_inc(q, 1)
            dve.wait_ge(q, 7 + TERMS)
            nc.vector.scalar_tensor_tensor(row(5), row(5), 1.0, row(3), ALU.add, ALU.mult).then_inc(q, 1)
            dve.wait_ge(q, SOFT)
            nc.vector.scalar_tensor_tensor(consts["k_half"][:, :], row(5), -8.0, row(6), ALU.mult, ALU.add)\
                .then_inc(q, 1)
            TS(consts["b_half"][:, :], b_gates[:, :], 0.5, None, ALU.mult).then_inc(q, 1)
            nc.vector.tensor_copy(consts["tri"][:, :], tri_raw[:, :]).then_inc(q, 1)
            layer1["first"](dve, "vector")
            dve.wait_ge(pool_set1, POOL_SET1 + 1)
            layer1["iterate"](dve, layer1["vector"])

        @block.scalar
        def _(act):
            act.wait_ge(loaded, LOADED)
            act.wait_ge(dve_set, DVE_SET)
            act.wait_ge(pool_set, POOL_SET)
            att["iterate"](act, att["scalar"])
            act.wait_ge(soft_step, 3)
            nc.scalar.activation(soft[:, 2, :], soft[:, 1, :], ACT.Exp, scale=-1.0).then_inc(soft_step, 1)
            act.wait_ge(soft_step, SOFT + 3)
            act.wait_ge(loaded1, LOADED1)
            layer1["first"](act, "scalar")
            layer1["iterate"](act, layer1["scalar"])

        @block.tensor
        def _(pe):
            pe.wait_ge(loaded, LOADED)
            pe.wait_ge(dve_set, DVE_SET)
            pe.wait_ge(pool_set, POOL_SET)
            att["iterate"](pe, att["tensor"])
            pe.wait_ge(soft_step, SOFT + 3)
            pe.wait_ge(loaded1, LOADED1)
            layer1["first"](pe, "tensor")
            layer1["iterate"](pe, layer1["tensor"])


def layouts(i):
    import numpy as np
    D = 128
    qkv = np.asarray(i["L0_attn_w_qkv"]).reshape(D, 8, 2, 8, 3)
    a = {"z": i["L0_attn_z"]}
    a["w_q"] = qkv[..., 0].transpose(0, 2, 3, 1).reshape(D, D)
    a["w_k"] = qkv[..., 1].transpose(0, 2, 3, 1).reshape(D, D)
    a["w_v"] = qkv[..., 2].reshape(D, D)
    a["w_proj"] = np.asarray(i["L0_attn_w_proj"]).reshape(2, 2, 4, 8, D).transpose(0, 2, 1, 3, 4).reshape(D, D)
    L1 = {n[8:]: np.asarray(v) for n, v in i.items() if n.startswith("L1_attn_")}
    for n in ("W_in", "W_gates", "W_out", "W_grow", "W_shrink"):
        a[n.lower()] = L1[n].T
    a["conv_w"] = L1["conv_w"].reshape(2, D, 4).transpose(1, 0, 2)
    for n in ("conv_b", "b_gates", "forget_base"):
        a[n] = L1[n].reshape(-1, D).T
    a["gamma1"], a["gamma2"] = L1["gamma1"], L1["gamma2"]
    for n in ("w_gate", "w_expert", "b_expert"):
        a[n] = i["L1_ffn_" + n]
    for new, old in (("ln_scale", "L0_attn_ln_scale"), ("ln_bias", "L0_attn_ln_bias"), ("b_proj", "L0_attn_b_proj"),
                     ("ffn_kernel", "L0_ffn_kernel"), ("s_in", "L0_ffn_input_scale"), ("s_k", "L0_ffn_kernel_scale"),
                     ("ffn_bias", "L0_ffn_bias")):
        a[new] = i[old]
    return {n: np.ascontiguousarray(v) for n, v in a.items()}


def kernel(**inputs):
    import concourse.bacc as bacc
    from concourse.bass_utils import run_bass_kernel_spmd

    nc = bacc.Bacc("TRN2", target_bir_lowering=False, num_devices=1)
    arrays = layouts(inputs)
    aps = {n: nc.dram_tensor(f"in_{n}_dram", v.shape, mybir.dt.from_np(v.dtype), kind="ExternalInput").ap()
           for n, v in arrays.items()}
    out = nc.dram_tensor("out_0_dram", arrays["z"].shape, F32, kind="ExternalOutput").ap()
    build(nc, aps, out)
    r = run_bass_kernel_spmd(nc, [{f"in_{n}_dram": v for n, v in arrays.items()}], core_ids=[0])
    return r.results[0]["out_0_dram"]
```

```python
from contextlib import ExitStack

import concourse.bass as bass
from concourse import mybir

ALU = mybir.AluOpType
ACT = mybir.ActivationFunctionType
AX_X = mybir.AxisListType.X
F32 = mybir.dt.float32
BF16 = mybir.dt.bfloat16
U32 = mybir.dt.uint32

P = 128
D = 128
EPS = 1e-5


def wait(eng, sem, value):
    if isinstance(value, int):
        if value > 0:
            eng.wait_ge(sem, value)
    else:
        eng.wait_ge(sem, value)


def wait_apart(eng, sem, value, past_wait):
    wait(eng, sem, value)
    if not isinstance(value, int):
        eng.sem_inc(past_wait, 1)


def bank_free(pe, i, live, uses, name):
    at = [u[0] for u in uses].index(name)
    for back in range(1, len(uses) * 4):
        j, n = (at - back) // len(uses), (at - back) % len(uses)
        _, off, read, per_batch, nth = uses[n]
        if live(i + j, off):
            wait(pe, read, per_batch * (i + j + off) + nth)
            return
        if isinstance(i, int) and i + j < -3:
            return


def raw_stats(nc, bn, src, raw, C):
    for c in range(C):
        nc.vector.bn_stats(bn[:, c, :], src(c)).then_inc(raw, 1)


def mean_var(nc, dve, bn, mv, raw, done, C, b, past_wait):
    wait_apart(dve, raw, C * (b + 1), past_wait)
    for c in range(C):
        nc.vector.bn_aggr(mv[:, c, :], bn[:, c, :]).then_inc(done, 1)


def norm_stats(nc, dve, src, bn, mv, raw, done, C, b, past_wait):
    raw_stats(nc, bn, src, raw, C)
    mean_var(nc, dve, bn, mv, raw, done, C, b, past_wait)


def attention_phase(nc, ctx, sems, psum, x_in, x_all, w, consts, NB):
    C = x_in.shape[1] // P
    T = x_in.shape[1]
    H, HD = 16, 8
    NP = H // 2
    SPLIT = 6
    Q_PART = (0, 0, 0, 1, 1, 2)
    K_PART = (0, 1, 2, 0, 1, 0)
    KROWS = SPLIT * HD
    MROWS = 3
    SCALE = float(1.0 / (D / H) ** 0.5)
    STACK_DMAS = 3 * SPLIT
    KSTACK_DMAS = SPLIT
    MROW_DMAS = 2

    def sb(name, shape, dt=F32):
        return ctx.enter_context(nc.sbuf_tensor(name, shape, dt))

    def sem(name):
        return ctx.enter_context(nc.semaphore(name))

    q_stack = [sb(f"q_stack{i}", [P, NP, T], BF16) for i in range(2)]
    k_stack = [sb(f"k_stack{i}", [P, NP, T], BF16) for i in range(2)]
    v_pad = [sb(f"v_pad{i}", [P, C, H, 32]) for i in range(2)]
    probs = sb("probs", [P, 2 * 4 * C, T])
    q_parts = sb("q_parts", [P, 3, T], BF16)
    k_parts = sb("k_parts", [P, 3, T], BF16)
    q_rest = sb("q_rest", [P, T])
    k_rest = sb("k_rest", [P, T])
    neg_max = [sb(f"neg_max{i}", [P, C, 4, 2]) for i in range(2)]
    max_rest = sb("max_rest", [P, C, 2, 4])
    max_parts = sb("max_parts", [P, C, 2, 3, 4], BF16)
    max_rows = sb("max_rows", [3 * 8, T], BF16)
    bn_a = sb("bn_a", [P, C, 6])
    mv_a = sb("mv_a", [P, C, 2])
    bn_b = sb("bn_b", [P, C, 6])
    mv_b = sb("mv_b", [P, C, 2])
    bn_c = sb("bn_c", [P, C, 6])
    mv_c = sb("mv_c", [P, C, 2])
    bn_d = sb("bn_d", [P, C, 6])
    mv_d = sb("mv_d", [P, C, 2])
    mean_rs = sb("mean_rs", [P, NB, 2, C])
    tiny = sb("tiny", [P, 8, C])
    tiny_bf = sb("tiny_bf", [P, 4, C], BF16)
    centred = sb("centred", [P, C, D])
    zn = sb("zn", [P, C, D])
    znT = sb("znT", [P, T])
    outT = [sb(f"outT{i}", [P, T]) for i in range(2)]
    rowsum_inv = sb("rowsum_inv", [P, C * 4 * 2])
    o_nat = sb("o_nat", [P, C, 2, 8, HD])
    oT = sb("oT", [P, T])
    z_res = sb("z_res", [P, C, D])
    att = sb("att", [P, C, D])
    att_c = centred
    y_bf = sb("y_bf", [P, C, D], BF16)
    y_scaled = sb("y_scaled", [P, C * D])
    y_grid = sb("y_grid", [P, C * D])
    y_sum = sb("y_sum", [P, C * D])
    y_q = sb("y_q", [P, C, D], BF16)
    y_absmax = sb("y_absmax", [P, C])
    poison = sb("poison", [P, C])
    yT = sb("yT", [P, T], BF16)
    f_bf = sb("f_bf", [P, C, D], BF16)
    f_b = sb("f_b", [P, C, D], BF16)
    f_c = sb("f_c", [P, C, D], BF16)

    score_ps = psum[0:2]
    st_ps = psum[2:4]
    acc = psum[4]
    misc = psum[5]
    misc_bf = misc[:, 0:T // 2].bitcast(BF16)

    x_loaded, past_wait = sems["x_loaded"], sems["past_wait"]
    names = ("stat_a stat_a_raw prep_step zn_ready znT_ps znT_ready q_ps q_hi q_r q_lo k_ps k_hi k_r k_lo "
             "stack_ready kstack_ready max_ps max_read max_split maxT_ps maxT_read mrow_ready st_ready exp_done pv_done "
             "acc_read o_ps rowsum_ready o_nat_ready oT_ps oT_ready v_ps v_ready zres_step proj_ps att_ready "
             "stat_b_raw stat_b x1_step stat_c_raw stat_c y_step quant_step yT_ps yT_ready ffn_ps ffn_read "
             "ffn_biased stat_d_raw stat_d x2_step").split()
    s = {n: sem(n) for n in names}
    sems.update(s)

    def live(i, off):
        return not isinstance(i, int) or 0 <= i + off < NB

    MISC = [("yT", -2, s["yT_ready"], 1, 1), ("ffn", -2, s["ffn_read"], 1, 1), ("maxT1", 0, s["maxT_read"], 2, 2),
            ("o1", -1, s["o_nat_ready"], 2, 2), ("v", 1, s["v_ready"], 2, 2), ("oT", -1, s["oT_ready"], 1, 1),
            ("proj", -1, s["att_ready"], 1, 1), ("znT", 2, s["znT_ready"], 1, 1), ("q", 2, s["q_r"], 1, 1),
            ("maxT0", 1, s["maxT_read"], 2, 1), ("k", 2, s["k_r"], 1, 1), ("o0", 0, s["o_nat_ready"], 2, 1)]

    def wait_misc_free(pe, i, name):
        bank_free(pe, i, live, MISC, name)

    def tensor(pe, i, par):
        def score_max(p, c):
            j, b, bpar = (p + 6) % NP, (i if p < 2 else i + 1), (par if p < 2 else 1 - par)
            if not live(b, 0):
                return
            if j == 0 and c == 0:
                wait(pe, s["stack_ready"], 16 * STACK_DMAS * (b + 1))
                wait(pe, s["kstack_ready"], 16 * KSTACK_DMAS * (b + 1))
            wait(pe, s["max_read"], 32 * b + 4 * j + c - 1)
            for h in range(2):
                rows = slice(64 * h, 64 * h + KROWS)
                mm = nc.tensor.matmul(score_ps[c % 2][:, h, :], q_stack[bpar][rows, j, c * P:(c + 1) * P],
                                      k_stack[bpar][rows, j, :], start=True, stop=True)
            mm.then_inc(s["max_ps"], 1)

        def score_t(p, c, h):
            if not live(i, 0):
                return
            if c == h == 0 and p in (0, 4):
                wait(pe, s["mrow_ready"], 16 * MROW_DMAS * (2 * i + 1 + p // 4))
            n = 64 * i + 8 * p + 2 * c + h + 1
            wait(pe, s["exp_done"], n - 2)
            rows = slice(64 * h, 64 * h + KROWS + MROWS)
            nc.tensor.matmul(st_ps[h][:, :], k_stack[par][rows, p, c * P:(c + 1) * P],
                             q_stack[par][rows, p, :], start=True, stop=True).then_inc(s["st_ready"], 1)

        def prob_v(p, c):
            b, a, bpar = (i - 1, 3, 1 - par) if p < 2 else (i, p // 2 - 1, par)
            if not live(b, 0):
                return
            kc = 2 * (p % 2) + c // 2
            u, t = a // 2, a % 2
            if a == 0 and kc == 0:
                wait(pe, s["v_ready"], 2 * b + 2)
            if t == 0 and kc == 0:
                wait(pe, s["acc_read"], 2 * b + u)
            wait(pe, s["exp_done"], 64 * b + 8 * (2 * a + 1) + 2 * kc + 2)
            for g in range(4):
                mm = nc.tensor.matmul(acc[32 * g:32 * g + 32, :], v_pad[bpar][:, kc, 4 * a + g, :],
                                      probs[:, (a % 2) * 4 * C + g * C + kc, :],
                                      start=(t == 0 and kc == 0), stop=(t == 1 and kc == C - 1),
                                      skip_group_check=True)
            mm.then_inc(s["pv_done"], 1)

        def transpose4(src, ident, out, n, done):
            for c in range(C):
                mm = nc.tensor.transpose(out[0:n, c * P:(c + 1) * P], src(c), ident)
            mm.then_inc(done, 1)

        def max_t(half, b):
            name = f"maxT{half}"
            wait(pe, s["max_split"], 4 * (2 * b + half + 1))
            wait_misc_free(pe, i, name)
            transpose4(lambda c: max_parts[:, c].rearrange("p s a j -> p (s a j)"), consts["ident_bf"][:, :],
                       misc_bf, 3 * 8, s["maxT_ps"])

        def out_nat(u, b):
            wait(pe, s["acc_read"], 2 * b + u + 1)
            wait_misc_free(pe, i, f"o{u}")
            transpose4(lambda c: outT[u][:, c * P:(c + 1) * P], consts["ident"][:, :], misc, P, s["o_ps"])

        def side_product(slot):
            if slot == 2 and live(i, -2):
                wait(pe, s["quant_step"], 10 * (i - 2) + 5)
                wait_misc_free(pe, i, "yT")
                transpose4(lambda c: y_q[:, c, :], consts["ident_bf"][:, :], misc_bf, P, s["yT_ps"])
            if slot == 3 and live(i, -2):
                wait(pe, s["yT_ready"], i - 2 + 1)
                wait_misc_free(pe, i, "ffn")
                for c in range(C):
                    mm = nc.tensor.matmul(misc[:, c * D:(c + 1) * D], yT[:, c * P:(c + 1) * P], w["ffn"][:, :],
                                          start=True, stop=True)
                mm.then_inc(s["ffn_ps"], 1)
            if slot == 4 and live(i, 0):
                max_t(1, i)
            if slot == 5 and live(i, -1):
                out_nat(1, i - 1)
            if slot == 6 and live(i, 1):
                wait(pe, s["znT_ready"], i + 1 + 1)
                wait_misc_free(pe, i, "v")
                for c in range(C):
                    mm = nc.tensor.matmul(misc[:, c * D:(c + 1) * D], znT[:, c * P:(c + 1) * P], w["v"][:, :],
                                          start=True, stop=True)
                mm.then_inc(s["v_ps"], 1)
            if slot == 7 and live(i, -1):
                wait(pe, s["o_nat_ready"], 2 * (i - 1) + 2)
                wait_misc_free(pe, i, "oT")
                transpose4(lambda c: o_nat[:, c].rearrange("p u g d -> p (u g d)"), consts["ident"][:, :],
                           misc, P, s["oT_ps"])
            if slot == 9 and live(i, 2):
                wait(pe, s["zn_ready"], i + 2 + 1)
                wait_misc_free(pe, i, "znT")
                transpose4(lambda c: zn[:, c, :], consts["ident"][:, :], misc, P, s["znT_ps"])
            if slot == 8 and live(i, -1):
                wait(pe, s["oT_ready"], i - 1 + 1)
                wait_misc_free(pe, i, "proj")
                for c in range(C):
                    mm = nc.tensor.matmul(misc[:, c * D:(c + 1) * D], oT[:, c * P:(c + 1) * P], w["proj"][:, :],
                                          start=True, stop=True)
                mm.then_inc(s["proj_ps"], 1)
            if slot in (11, 13) and live(i, 2):
                n = "q" if slot == 11 else "k"
                wait(pe, s["znT_ready"], i + 2 + 1)
                wait_misc_free(pe, i, n)
                nc.tensor.matmul(misc[:, :], w[n][:, :], znT[:, :], start=True, stop=True).then_inc(s[n + "_ps"], 1)
            if slot == 12 and live(i, 1):
                max_t(0, i + 1)
            if slot == 14 and live(i, 0):
                out_nat(0, i)

        for p in range(NP):
            for c in range(0, C, 2):
                score_t(p, c, 0)
                score_max(p, c)
                score_t(p, c, 1)
                score_max(p, c + 1)
                score_t(p, c + 1, 0)
                prob_v(p, c + 1)
                score_t(p, c + 1, 1)
                side_product(2 * p + c // 2)

    def scalar(act, i, par):
        def side_read(slot):
            if slot == 2 and live(i, -2):
                wait(act, s["yT_ps"], i - 2 + 1)
                wait(act, s["ffn_ps"], i - 2)
                nc.scalar.activation(yT[:, :], misc_bf, ACT.Copy).then_inc(s["yT_ready"], 1)
            for at, u, off in ((3, 1, -1), (11, 0, 0)):
                if slot == at and live(i, off):
                    b = i + off
                    wait(act, s["pv_done"], 16 * b + 8 * (u + 1))
                    wait(act, s["o_ps"], 2 * (b - 1) + u + 1)
                    nc.scalar.activation(outT[u][:, :], acc[:, :], ACT.Copy).then_inc(s["acc_read"], 1)
            if slot == 3 and live(i, -2):
                wait(act, s["ffn_ps"], i - 2 + 1)
                wait(act, s["ffn_biased"], i - 2)
                nc.scalar.activation(f_bf[:, :, :].rearrange("p c d -> p (c d)"), misc[:, :], ACT.Identity,
                                     bias=0.0, scale=consts["s_both"][:, 0:1]).then_inc(s["ffn_read"], 1)
            for at, half, off in ((4, 1, 0), (12, 0, 1)):
                if slot == at and live(i, off):
                    n = 2 * (i + off) + half
                    wait(act, s["maxT_ps"], n + 1)
                    wait(act, s["mrow_ready"], 16 * MROW_DMAS * n)
                    nc.scalar.activation(max_rows[:, :], misc_bf[0:3 * 8, :], ACT.Copy).then_inc(s["maxT_read"], 1)
            if slot == 6 and live(i, 1):
                wait(act, s["v_ps"], i + 1 + 1)
                wait(act, s["pv_done"], 16 * (i - 1) + 16)
                src = misc[:, :].rearrange("p (cu t g d) -> p cu t g d", t=2, g=4, d=HD)
                dst = v_pad[1 - par][:, :, :, :].rearrange("p c (u t g) e -> p (c u) t g e", u=2, t=2)
                for t in range(2):
                    nc.scalar.activation(dst[:, :, t, :, 16 * t:16 * t + HD], src[:, :, t], ACT.Copy)\
                        .then_inc(s["v_ready"], 1)
            if slot == 7 and live(i, -1):
                wait(act, s["oT_ps"], i - 1 + 1)
                wait(act, s["proj_ps"], i - 1)
                nc.scalar.activation(oT[:, :], misc[:, :], ACT.Copy).then_inc(s["oT_ready"], 1)
            if slot == 9 and live(i, 2):
                wait(act, s["znT_ps"], i + 2 + 1)
                wait(act, s["k_ps"], i + 2)
                wait(act, s["v_ps"], i + 2)
                nc.scalar.activation(znT[:, :], misc[:, :], ACT.Identity, bias=consts["ln_bias"][:, 0:1],
                                     scale=consts["ln_scale"][:, 0:1]).then_inc(s["znT_ready"], 1)
            if slot in (11, 13) and live(i, 2):
                n, parts = ("q", q_parts) if slot == 11 else ("k", k_parts)
                wait(act, s[n + "_ps"], i + 2 + 1)
                wait(act, s["stack_ready"], 16 * STACK_DMAS * (i + 2))
                wait(act, s["kstack_ready"], 16 * KSTACK_DMAS * (i + 2))
                nc.scalar.activation(parts[:, 0, :], misc[:, :], ACT.Copy).then_inc(s[n + "_hi"], 1)

        for p in range(NP):
            for c in range(C):
                if live(i, 0):
                    for h in range(2):
                        wait(act, s["st_ready"], 64 * i + 8 * p + 2 * c + h + 1)
                        wait(act, s["pv_done"], 16 * i + 4 * (p // 2) + c + 1 - 8)
                        nc.scalar.activation(probs[:, (p // 2 % 2) * 4 * C + (2 * (p % 2) + h) * C + c, :],
                                             st_ps[h][:, :], ACT.Exp, scale=SCALE).then_inc(s["exp_done"], 1)
                if c % 2:
                    side_read(2 * p + c // 2)

    def vector(dve, i, par):
        def side(slot):
            for at, half, off in ((3, 1, 0), (11, 0, 1)):
                if slot == at and live(i, off):
                    n = 2 * (i + off) + half
                    m = neg_max[half][:, :, :, :].rearrange("p c j s -> p c s j")
                    rest = max_rest[:, :, :, :]
                    wait(dve, s["max_read"], 16 * (n + 1))
                    wait(dve, s["maxT_ps"], n)
                    nc.vector.tensor_copy(max_parts[:, :, :, 0], m).then_inc(s["max_split"], 1)
                    wait(dve, s["max_split"], 4 * n + 1)
                    nc.vector.tensor_tensor(rest, m, max_parts[:, :, :, 0], ALU.subtract).then_inc(s["max_split"], 1)
                    wait(dve, s["max_split"], 4 * n + 2)
                    nc.vector.tensor_copy(max_parts[:, :, :, 1], rest).then_inc(s["max_split"], 1)
                    wait(dve, s["max_split"], 4 * n + 3)
                    nc.vector.tensor_tensor(max_parts[:, :, :, 2], rest, max_parts[:, :, :, 1], ALU.subtract)\
                        .then_inc(s["max_split"], 1)
            if slot == 2 and live(i, 2):
                b = i + 2
                wait(dve, x_loaded, 16 * (b + 1))
                wait(dve, s["prep_step"], 9 * b)
                raw_stats(nc, bn_a, lambda c: x_all[:, b, c * D:(c + 1) * D], s["stat_a_raw"], C)
            for at, u, off in ((5, 1, -1), (14, 0, 0)):
                if slot == at and live(i, off):
                    n = 2 * (i + off) + u
                    o = misc[:, :].rearrange("p (g e) -> p g e", e=16)
                    wait(dve, s["o_ps"], n + 1)
                    wait(dve, s["o_nat_ready"], n)
                    nc.vector.reciprocal(rowsum_inv[:, :], o[:, :, HD:HD + 1].rearrange("p g e -> p (g e)"))\
                        .then_inc(s["rowsum_ready"], 1)
                    wait(dve, s["rowsum_ready"], n + 1)
                    wait(dve, s["oT_ps"], i + off)
                    nc.vector.tensor_tensor(
                        o_nat[:, :, u], o[:, :, 0:HD].rearrange("p (c g) d -> p c g d", c=C),
                        rowsum_inv[:, :].rearrange("p (c g) -> p c g", c=C).unsqueeze(3).to_broadcast([P, C, 8, HD]),
                        ALU.mult).then_inc(s["o_nat_ready"], 1)
            if slot == 8 and live(i, -1):
                b = i - 1
                wait(dve, s["proj_ps"], b + 1)
                wait(dve, s["zres_step"], 3 * (b + 1))
                wait(dve, s["x1_step"], 5 * b)
                nc.vector.tensor_tensor(att[:, :, :].rearrange("p c d -> p (c d)"), misc[:, :],
                                        z_res[:, :, :].rearrange("p c d -> p (c d)"), ALU.add)\
                    .then_inc(s["att_ready"], 1)
            if slot == 9 and live(i, -1):
                b = i - 1
                wait(dve, s["att_ready"], b + 1)
                wait(dve, s["x1_step"], 5 * b)
                raw_stats(nc, bn_b, lambda c: att[:, c, :], s["stat_b_raw"], C)
            if slot == 12 and live(i, -1):
                b = i - 1
                wait(dve, s["x1_step"], 5 * (b + 1))
                wait(dve, s["y_step"], 4 * b)
                raw_stats(nc, bn_c, lambda c: x_all[:, b, c * D:(c + 1) * D], s["stat_c_raw"], C)
            q = s["quant_step"]
            if slot == 15 and live(i, -1):
                b = i - 1
                wait(dve, s["y_step"], 4 * (b + 1))
                nc.vector.tensor_scalar(y_scaled[:, :], y_bf[:, :, :].rearrange("p c d -> p (c d)"),
                                        consts["s_in_inv"][:, 0:1], None, ALU.mult).then_inc(q, 1)
                wait(dve, q, 10 * b + 1)
                nc.vector.tensor_scalar(y_grid[:, :].bitcast(U32), y_scaled[:, :].bitcast(U32), 0x7F800000, None,
                                        ALU.bitwise_and).then_inc(q, 1)
            if slot == 0 and live(i, -2):
                b = i - 2
                wait(dve, q, 10 * b + 3)
                nc.vector.tensor_tensor(y_sum[:, :], y_scaled[:, :], y_grid[:, :], ALU.add).then_inc(q, 1)
            if slot == 1 and live(i, -2):
                b = i - 2
                wait(dve, q, 10 * b + 4)
                wait(dve, s["yT_ps"], b)
                nc.vector.tensor_tensor(y_q[:, :, :].rearrange("p c d -> p (c d)"), y_sum[:, :], y_grid[:, :],
                                        ALU.subtract).then_inc(q, 1)
            if slot == 4 and live(i, -2):
                nc.vector.tensor_reduce(y_absmax[:, :], y_scaled[:, :].rearrange("p (c d) -> p c d", c=C), AX_X,
                                        ALU.max, apply_absolute_value=True).then_inc(q, 1)
            if slot == 4 and live(i, -2):
                b = i - 2
                wait(dve, s["ffn_read"], b + 1)
                wait(dve, s["x2_step"], 10 * b)
                nc.vector.tensor_tensor(f_b[:, :, :], f_bf[:, :, :],
                                        consts["ffn_bias"][:, :].unsqueeze(1).to_broadcast([P, C, D]), ALU.add)\
                    .then_inc(s["ffn_biased"], 1)
            if slot == 6 and live(i, -2):
                b = i - 2
                wait(dve, s["ffn_biased"], b + 1)
                raw_stats(nc, bn_d, lambda c: f_b[:, c, :], s["stat_d_raw"], C)

        def between(slot):
            if slot in (12, 14) and live(i, 2):
                n, parts, rest = ("q", q_parts, q_rest) if slot == 12 else ("k", k_parts, k_rest)
                wait(dve, s[n + "_hi"], i + 2 + 1)
                wait(dve, s[n + "_lo"], 2 * (i + 2))
                nc.vector.tensor_tensor(rest[:, :], misc[:, :], parts[:, 0, :], ALU.subtract)\
                    .then_inc(s[n + "_r"], 1)
            q = s["quant_step"]
            if slot == 0 and live(i, -2):
                b = i - 2
                wait(dve, q, 10 * b + 2)
                nc.vector.tensor_scalar(y_grid[:, :], y_grid[:, :], 2.0 ** -6, 1.5 * 2.0 ** 20, ALU.max, ALU.mult)\
                    .then_inc(q, 1)
            if slot == 5 and live(i, -2):
                b = i - 2
                wait(dve, q, 10 * b + 6)
                nc.vector.tensor_scalar(y_absmax[:, :], y_absmax[:, :], 464.0, 464.0, ALU.max, ALU.subtract)\
                    .then_inc(q, 1)
            if slot == 6 and live(i, -2):
                b = i - 2
                wait(dve, q, 10 * b + 7)
                nc.vector.tensor_scalar(y_absmax[:, :], y_absmax[:, :], 1e30, 1e30, ALU.mult, ALU.mult)\
                    .then_inc(q, 2)
            if slot == 7 and live(i, -2):
                b = i - 2
                wait(dve, q, 10 * b + 9)
                wait(dve, s["x2_step"], 10 * b)
                nc.vector.tensor_scalar(poison[:, :], y_absmax[:, :], 1e30, None, ALU.mult).then_inc(q, 1)
            for at, name, off, bn, mv in ((3, "stat_a", 2, bn_a, mv_a), (7, "stat_d", -2, bn_d, mv_d),
                                          (10, "stat_b", -1, bn_b, mv_b), (13, "stat_c", -1, bn_c, mv_c)):
                if slot == at and live(i, off):
                    mean_var(nc, dve, bn, mv, s[name + "_raw"], s[name], C, i + off, past_wait)

        for p in range(NP):
            j, b = (p + 6) % NP, (i if p < 2 else i + 1)
            for c in range(C):
                if live(b, 0):
                    wait(dve, s["max_ps"], 32 * b + 4 * j + c + 1)
                    if j % 4 == 0 and c == 0:
                        wait(dve, s["max_split"], 4 * (2 * (b - 1) + j // 4 + 1))
                    nc.vector.tensor_reduce(neg_max[j // 4][:, c, j % 4, :], score_ps[c % 2][:, :, :], AX_X, ALU.max,
                                            negate=True).then_inc(s["max_read"], 1)
                (side if c % 2 else between)(2 * p + c // 2)

    def per_token(x):
        return x.unsqueeze(2).to_broadcast([P, C, D])

    def pool(gp, i, par):
        if live(i, 1):
            b = i + 1
            wait_apart(gp, s["k_lo"], 2 * (b + 1), past_wait)
            wait_apart(gp, s["st_ready"], 64 * b - 64, past_wait)
            for r, part in enumerate(K_PART):
                gp.dma_start(k_stack[1 - par][64 + HD * r:64 + HD * (r + 1), :, :], k_parts[64:128, part, :])\
                    .then_inc(s["kstack_ready"], 16)
        TT, TS = nc.gpsimd.tensor_tensor, nc.gpsimd.tensor_scalar
        t = lambda n: tiny[:, n, :]
        half_neg, half = consts["pow"][:, 0, :], consts["pow"][:, 1, :]
        neg_one = consts["pow"][:, 2, :]

        def x_of(b):
            return x_all[:, b, :].rearrange("p (c d) -> p c d", c=C)

        if live(i, 2):
            b = i + 2
            q, at0 = s["prep_step"], 9 * b
            wait_apart(gp, s["stat_a"], C * (b + 1), past_wait)
            TS(t(0), mv_a[:, :, 1], EPS, None, ALU.add).then_inc(q, 1)
            nc.gpsimd.tensor_copy(mean_rs[:, b, 0, :], mv_a[:, :, 0]).then_inc(q, 1)
            wait_apart(gp, q, at0 + 1, past_wait)
            TT(mean_rs[:, b, 1, :], t(0), half_neg, ALU.pow).then_inc(q, 1)
            wait_apart(gp, q, at0 + 3, past_wait)
            TT(t(1), mv_a[:, :, 1], mean_rs[:, b, 1, :], ALU.mult).then_inc(q, 1)
            wait_apart(gp, q, at0 + 4, past_wait)
            TT(t(2), t(1), mean_rs[:, b, 1, :], ALU.mult).then_inc(q, 1)
            wait_apart(gp, q, at0 + 5, past_wait)
            TS(t(3), t(2), EPS, None, ALU.add).then_inc(q, 1)
            wait_apart(gp, q, at0 + 6, past_wait)
            TT(t(4), t(3), half_neg, ALU.pow).then_inc(q, 1)
            wait_apart(gp, q, at0 + 7, past_wait)
            TT(t(5), t(4), mean_rs[:, b, 1, :], ALU.mult).then_inc(q, 1)
            wait_apart(gp, s["y_step"], 4 * (b - 3), past_wait)
            TT(centred[:, :, :], x_of(b), per_token(mean_rs[:, b, 0, :]), ALU.subtract).then_inc(q, 1)
            wait_apart(gp, q, at0 + 9, past_wait)
            wait_apart(gp, s["znT_ps"], b, past_wait)
            TT(zn[:, :, :], centred[:, :, :], per_token(t(5)), ALU.mult).then_inc(s["zn_ready"], 1)
        if live(i, -1):
            b = i - 1
            q, at0 = s["zres_step"], 3 * b
            wait_apart(gp, s["att_ready"], b, past_wait)
            TT(z_res[:, :, :], x_of(b), per_token(mean_rs[:, b, 0, :]), ALU.subtract).then_inc(q, 1)
            wait_apart(gp, q, at0 + 1, past_wait)
            TT(z_res[:, :, :], z_res[:, :, :], per_token(mean_rs[:, b, 1, :]), ALU.mult).then_inc(q, 1)
            wait_apart(gp, q, at0 + 2, past_wait)
            TT(z_res[:, :, :], z_res[:, :, :], consts["b_proj"][:, :].unsqueeze(1).to_broadcast([P, C, D]),
               ALU.add).then_inc(q, 1)

        if live(i, -2):
            b = i - 2
            q, at0 = s["x2_step"], 10 * b
            wait_apart(gp, s["stat_d"], C * (b + 1), past_wait)
            nc.gpsimd.tensor_copy(tiny_bf[:, 0, :], mv_d[:, :, 0]).then_inc(q, 1)
            nc.gpsimd.tensor_copy(tiny_bf[:, 1, :], mv_d[:, :, 1]).then_inc(q, 1)
            wait_apart(gp, q, at0 + 2, past_wait)
            TT(f_c[:, :, :], f_b[:, :, :], per_token(tiny_bf[:, 0, :]), ALU.subtract).then_inc(q, 1)
            TS(tiny_bf[:, 2, :], tiny_bf[:, 1, :], EPS, None, ALU.add).then_inc(q, 1)
            wait_apart(gp, q, at0 + 4, past_wait)
            TT(tiny_bf[:, 3, :], tiny_bf[:, 2, :], half, ALU.pow).then_inc(q, 1)
            wait_apart(gp, q, at0 + 5, past_wait)
            TT(t(6), tiny_bf[:, 3, :], neg_one, ALU.pow).then_inc(q, 1)
            wait_apart(gp, q, at0 + 6, past_wait)
            TT(t(7), t(6), poison[:, :], ALU.add).then_inc(q, 1)
            wait_apart(gp, q, at0 + 7, past_wait)
            TT(f_c[:, :, :], f_c[:, :, :], per_token(t(7)), ALU.mult).then_inc(q, 1)
            wait_apart(gp, q, at0 + 8, past_wait)
            TT(x_of(b), x_of(b), f_c[:, :, :], ALU.add).then_inc(q, 2)
        def split(n, parts, rest):
            b = i + 2
            wait_apart(gp, s[n + "_r"], b + 1, past_wait)
            TS(parts[:, 1, :], rest[:, :], 1.0, None, ALU.mult).then_inc(s[n + "_lo"], 1)
            wait_apart(gp, s[n + "_lo"], 2 * b + 1, past_wait)
            TT(parts[:, 2, :], rest[:, :], parts[:, 1, :], ALU.subtract).then_inc(s[n + "_lo"], 1)

        if live(i, -1):
            b = i - 1
            q, at0 = s["x1_step"], 5 * b
            wait_apart(gp, s["stat_b"], C * (b + 1), past_wait)
            TS(t(0), mv_b[:, :, 1], EPS, None, ALU.add).then_inc(q, 1)
            wait_apart(gp, s["zn_ready"], min(b + 4, NB) if isinstance(b, int) else b + 4, past_wait)
            TT(att_c[:, :, :], att[:, :, :], per_token(mv_b[:, :, 0]), ALU.subtract).then_inc(q, 1)
            wait_apart(gp, q, at0 + 2, past_wait)
            TT(t(1), t(0), half_neg, ALU.pow).then_inc(q, 1)
            wait_apart(gp, q, at0 + 3, past_wait)
            TT(att_c[:, :, :], att_c[:, :, :], per_token(t(1)), ALU.mult).then_inc(q, 1)
            wait_apart(gp, q, at0 + 4, past_wait)
            TT(x_of(b), x_of(b), att_c[:, :, :], ALU.add).then_inc(q, 1)
        if live(i, 2):
            split("q", q_parts, q_rest)
        if live(i, -1):
            b = i - 1
            q, at0 = s["y_step"], 4 * b
            wait_apart(gp, s["stat_c"], C * (b + 1), past_wait)
            TS(t(0), mv_c[:, :, 1], EPS, None, ALU.add).then_inc(q, 1)
            TT(att_c[:, :, :], x_of(b), per_token(mv_c[:, :, 0]), ALU.subtract).then_inc(q, 1)
            wait_apart(gp, q, at0 + 2, past_wait)
            TT(t(1), t(0), half_neg, ALU.pow).then_inc(q, 1)
            wait_apart(gp, q, at0 + 3, past_wait)
            wait_apart(gp, s["quant_step"], 10 * b, past_wait)
            TT(y_bf[:, :, :], att_c[:, :, :], per_token(t(1)), ALU.mult).then_inc(q, 1)
        if live(i, 2):
            split("k", k_parts, k_rest)

    def sync(sp, i, par):
        if live(i, 2):
            wait_apart(sp, x_loaded, 16 * (i + 2), past_wait)
            sp.dma_start(x_all[:, i + 2, :].rearrange("p (c d) -> p c d", c=C),
                         x_in[i + 2].rearrange("(c p) d -> p c d", p=P)).then_inc(x_loaded, 16)
        if live(i, 1):
            b = i + 1
            wait_apart(sp, s["st_ready"], 64 * b - 64, past_wait)
            for done, parts, stack, order, halves in ((s["q_lo"], q_parts, q_stack[1 - par], Q_PART, 2),
                                                      (s["k_lo"], k_parts, k_stack[1 - par], K_PART, 1)):
                wait_apart(sp, done, 2 * (b + 1), past_wait)
                for h in range(halves):
                    for r, part in enumerate(order):
                        sp.dma_start(stack[64 * h + HD * r:64 * h + HD * (r + 1), :, :],
                                     parts[64 * h:64 * h + 64, part, :]).then_inc(s["stack_ready"], 16)
        for half, off in ((1, 0), (0, 1)):
            if live(i, off):
                n = 2 * (i + off) + half
                wait_apart(sp, s["maxT_read"], n + 1, past_wait)
                wait_apart(sp, s["mrow_ready"], 16 * MROW_DMAS * n, past_wait)
                for h in range(2):
                    sp.dma_start(q_stack[par ^ off][64 * h + KROWS:64 * h + KROWS + MROWS, 4 * half:4 * half + 4, :],
                                 max_rows[12 * h:12 * h + 12, :])\
                        .then_inc(s["mrow_ready"], 16)

    def iterate(eng, step):
        for i in range(-2, 4):
            step(eng, i, i % 2)
        with eng.Fori(0, NB // 2 - 3) as two:
            step(eng, two * 2 + 4, 0)
            step(eng, two * 2 + 5, 1)
        for i in range(NB - 2, NB):
            step(eng, i, i % 2)

    def tail(eng, step, i):
        step(eng, i, i % 2)

    return {"tensor": tensor, "scalar": scalar, "vector": vector, "pool": pool, "sync": sync, "tail": tail,
            "iterate": iterate, "k_stacks": k_stack, "v_pad": v_pad, "probs": probs, "zn": zn}


def hawk_moe_phase(nc, ctx, sems, psum, x_all, slots, padded, acc_y, w, consts, out, NB, T):
    C = T // P
    E = consts["rev"].shape[2]
    CAPACITY = 100
    TAPS = 4
    assert NB * C <= 256

    def sb(name, shape, dt=F32):
        return ctx.enter_context(nc.sbuf_tensor(name, shape, dt))

    two = lambda n: slots[:, n:n + 2, :]
    one = lambda n: slots[:, n, :]
    conv, gate_g = (two(0), two(2)), (two(4), two(6))
    tan_f, inp, grown, alpha, beta, h, gh = (two(n) for n in (8, 10, 12, 16, 18, 20, 22))
    zx = (one(24), one(29))
    xn, xn2, t, h4, y, xT, xn2T, h4T = (one(n) for n in (14, 25, 26, 27, 28, 15, 30, 31))
    xc_pad = padded[:, 0:2 * (T + TAPS - 1)].rearrange("p (n t) -> p n t", n=2)
    stats = {n: (sb(f"bn_{n}", [P, C, 6]), sb(f"mv_{n}", [P, C, 2])) for n in ("h", "t", "x3", "y")}
    stats["x2_0"], stats["x2_1"] = [(sb(f"bn_x2_{k}", [P, C, 6]), sb(f"mv_x2_{k}", [P, C, 2])) for k in range(2)]
    rs_x2 = [sb(f"rs_x2_{k}", [P, 4, C]) for k in range(2)]
    rs = {n: sb(f"rs_{n}", [P, 3, C]) for n in ("h", "t", "x3", "y")}
    top = sb("top", [P, 8, C])
    exps = sb("exps", [P, C, E])
    shifted = sb("shifted", [P, C, E])
    ranked = sb("ranked", [P, C, E])
    placed = sb("placed", [P, C, E])
    chosen = sb("chosen", [P, C, E], BF16)
    counts = sb("counts", [P, E], BF16)
    counted = sb("counted", [P, E])

    pair0, pair1, bank_t, bank_o, bank_y, bank_r = psum
    log_ps = bank_r[:, 0:C * E]
    cum_ps = bank_r[:, 2 * C * E:3 * C * E]

    names = ("stat_x2_raw stat_x2 rs_x2_step xn_step xn_ready xT_ps xT_ready xc_ps xc_copied conv_init conv_step gate_ps gate_ready "
             "forget_ps tanf_ready alpha_ready sq_ready om_ready beta_ready inp_ps inp_tanh u_ready xs_ready h_ready "
             "gh_ready z3_ready wout_ps xh_ready stat_h_raw stat_h rs_h_step xn2_ready xn2T_ps xn2T_ready "
             "mg_ps mg_ready mx_ps grown_ready shrink_ps t_ready stat_t_raw stat_t rs_t_step tn_ready x3_ready "
             "stat_x3_raw stat_x3 rs_x3_step h4_ready h4T_ps h4T_ready y_ps y_ready stat_y_raw stat_y rs_y_step logits_ps "
             "top_step exps_ready route_step count_step cum_ready place_step yc_ready yn_ready x4_ready").split()
    s = {n: ctx.enter_context(nc.semaphore("l1_" + n)) for n in names}
    past_wait = sems["past_wait"]

    def live(i, off):
        return not isinstance(i, int) or 0 <= i + off < NB

    PAIR0 = [("forget", -1, s["tanf_ready"], 2, 2), ("xc", 0, s["conv_init"], 2, 2), ("gate", 0, s["gate_ready"], 1, 1)]
    PAIR1 = [("inp", -1, s["inp_tanh"], 2, 2), ("mg", -2, s["mg_ready"], 1, 1), ("mx", -2, s["grown_ready"], 1, 1)]
    BANK_T = [("xT", 0, s["xT_ready"], 1, 1), ("xn2T", -2, s["xn2T_ready"], 1, 1), ("h4T", -3, s["h4T_ready"], 1, 1)]
    BANK_Y = [("y", -4, s["y_ready"], 1, 1), ("shrink", -3, s["t_ready"], 1, 1)]

    def tensor(pe, i, par):
        def transpose4(src, done):
            for c in range(C):
                mm = nc.tensor.transpose(bank_t[:, c * P:(c + 1) * P], src[:, c * P:(c + 1) * P],
                                         consts["ident"][:, :])
            mm.then_inc(done, 1)

        def two_chunks(dst, weight, first, src, done):
            K = len(src)
            for n in range(2):
                for k in range(K):
                    mm = nc.tensor.matmul(dst[:, n, :], weight[:, k, (first + n) * P:(first + n + 1) * P], src[k],
                                          start=(k == 0), stop=(k == K - 1))
            mm.then_inc(done, 1)

        def natural(dst, src, weight, done):
            for c in range(C):
                for k in range(2):
                    mm = nc.tensor.matmul(dst[:, c * D:(c + 1) * D], src[:, k, c * P:(c + 1) * P], weight[:, k, :],
                                          start=(k == 0), stop=(k == 1))
            mm.then_inc(done, 1)

        def forget_or_inp(name, dst, uses, first, b):
            cv = conv[(par + 1) & 1]
            wait(pe, s["conv_step"], 2 * (TAPS - 1) * (b + 1))
            bank_free(pe, i, live, uses, name)
            two_chunks(dst, w["gates"], first, [cv[:, k, :] for k in range(2)], s[name + "_ps"])

        if live(i, -1):
            forget_or_inp("forget", pair0, PAIR0, 0, i - 1)
        if live(i, -4):
            b = i - 4
            wait(pe, s["h4T_ready"], b + 1)
            wait(pe, s["top_step"], 2 * b)
            wait(pe, s["place_step"], 3 * b - 2)
            for c in range(C):
                mm = nc.tensor.matmul(log_ps[:, c * E:(c + 1) * E], h4T[:, c * P:(c + 1) * P], w["route"][:, :],
                                      start=True, stop=True)
            mm.then_inc(s["logits_ps"], 1)
            bank_free(pe, i, live, BANK_Y, "y")
            for c in range(C):
                mm = nc.tensor.matmul(bank_y[:, c * D:(c + 1) * D], h4T[:, c * P:(c + 1) * P], w["expert"][:, :],
                                      start=True, stop=True)
            mm.then_inc(s["y_ps"], 1)
        if live(i, -2):
            b = i - 2
            wait(pe, s["gh_ready"], b + 1)
            wait(pe, s["xh_ready"], b)
            natural(bank_o, gh, w["out"], s["wout_ps"])
        if live(i, -3):
            b = i - 3
            wait(pe, s["grown_ready"], b + 1)
            bank_free(pe, i, live, BANK_Y, "shrink")
            natural(bank_y, grown, w["shrink"], s["shrink_ps"])
        if live(i, 0):
            wait(pe, s["xn_ready"], i + 1)
            bank_free(pe, i, live, BANK_T, "xT")
            transpose4(xn, s["xT_ps"])
        if live(i, -1):
            forget_or_inp("inp", pair1, PAIR1, 2, i - 1)
        if live(i, -2):
            b = i - 2
            wait(pe, s["xn2_ready"], b + 1)
            bank_free(pe, i, live, BANK_T, "xn2T")
            transpose4(xn2, s["xn2T_ps"])
        if live(i, 0):
            wait(pe, s["xT_ready"], i + 1)
            bank_free(pe, i, live, PAIR0, "xc")
            two_chunks(pair0, w["in"], 2, [xT], s["xc_ps"])
        if live(i, -4):
            b = i - 4
            wait(pe, s["route_step"], 8 * b + 3)
            wait(pe, s["count_step"], 2 * b)
            wait(pe, s["place_step"], 3 * b)
            nc.tensor.matmul(cum_ps, consts["tri"][:, :], chosen[:, :, :].rearrange("p c e -> p (c e)"),
                             start=True, stop=False, skip_group_check=True)
            for c in range(C - 1):
                later = bank_r[:, 2 * C * E + (c + 1) * E:3 * C * E]
                nc.tensor.matmul(later, consts["ones"][:, :],
                                 chosen[:, c:c + 1, :].to_broadcast([P, C - 1 - c, E]),
                                 start=False, stop=False, skip_group_check=True)
            nc.tensor.matmul(cum_ps, consts["ones"][:, :], counts[:, :].unsqueeze(1).to_broadcast([P, C, E]),
                             start=False, stop=True, skip_group_check=True).then_inc(s["cum_ready"], 1)
        if live(i, -2):
            b = i - 2
            wait(pe, s["xn2T_ready"], b + 1)
            bank_free(pe, i, live, PAIR1, "mg")
            two_chunks(pair1, w["grow"], 0, [xn2T], s["mg_ps"])
        if live(i, 0):
            bank_free(pe, i, live, PAIR0, "gate")
            two_chunks(pair0, w["in"], 0, [xT], s["gate_ps"])
        if live(i, -2):
            bank_free(pe, i, live, PAIR1, "mx")
            two_chunks(pair1, w["grow"], 2, [xn2T], s["mx_ps"])
        if live(i, -3):
            b = i - 3
            wait(pe, s["h4_ready"], C * (b + 1))
            bank_free(pe, i, live, BANK_T, "h4T")
            transpose4(h4, s["h4T_ps"])

    def scalar(act, i, par):
        A = nc.scalar.activation
        if live(i, -1):
            b = i - 1
            wait(act, s["forget_ps"], b + 1)
            wait(act, s["alpha_ready"], 2 * b)
            for n in range(2):
                A(tan_f[:, n, :], pair0[:, n, :], ACT.Tanh, bias=consts["b_half"][:, n:n + 1], scale=0.5)\
                    .then_inc(s["tanf_ready"], 1)
            wait(act, s["h_ready"], 2 * b)
            wait(act, s["sq_ready"], b)
            for n in range(2):
                wait(act, s["tanf_ready"], 2 * b + n + 1)
                A(alpha[:, n, :], tan_f[:, n, :], ACT.Exp, bias=consts["k_half"][:, n:n + 1],
                  scale=consts["k_half"][:, n:n + 1]).then_inc(s["alpha_ready"], 1)
            wait(act, s["alpha_ready"], 2 * (b + 1))
            wait(act, s["xs_ready"], b)
            A(beta, alpha, ACT.Square).then_inc(s["sq_ready"], 1)
        if live(i, -4):
            b = i - 4
            wait(act, s["top_step"], 2 * (b + 1))
            wait(act, s["route_step"], 8 * b)
            A(exps[:, :, :], shifted[:, :, :], ACT.Exp).then_inc(s["exps_ready"], 1)
        if live(i, 0):
            wait(act, s["xT_ps"], i + 1)
            wait(act, s["gate_ps"], i)
            A(xT, bank_t[:, :], ACT.Copy, scale=consts["gamma1"][:, 0:1]).then_inc(s["xT_ready"], 1)
        if live(i, -1):
            b = i - 1
            wait(act, s["inp_ps"], b + 1)
            for n in range(2):
                A(inp[:, n, :], pair1[:, n, :], ACT.Tanh, bias=consts["b_half"][:, 2 + n:3 + n], scale=0.5)\
                    .then_inc(s["inp_tanh"], 1)
        if live(i, -1):
            b = i - 1
            wait(act, s["rs_x2_step"], 5 * (b + 1))
            wait(act, s["t_ready"], b - 1)
            wait(act, s["xn2_ready"], b - 1)
            for c in range(C):
                A(zx[(par + 1) & 1][:, c * D:(c + 1) * D], x_all[:, b, c * D:(c + 1) * D], ACT.Identity,
                  bias=rs_x2[(par + 1) & 1][:, 3, c:c + 1], scale=rs_x2[(par + 1) & 1][:, 1, c:c + 1])\
                    .then_inc(s["z3_ready"], 1)
        if live(i, -2):
            b = i - 2
            wait(act, s["xn2T_ps"], b + 1)
            wait(act, s["mx_ps"], b)
            A(xn2T, bank_t[:, :], ACT.Copy, scale=consts["gamma2"][:, 0:1]).then_inc(s["xn2T_ready"], 1)
        if live(i, 0):
            nc.scalar.preload_act_table_set("gelu_and_others")
            wait(act, s["xc_ps"], i + 1)
            wait(act, s["conv_step"], 2 * (TAPS - 1) * i)
            A(xc_pad[:, :, TAPS - 1:], pair0[:, :, :], ACT.Copy).then_inc(s["xc_copied"], 1)
            wait(act, s["inp_ps"], i - 1)
            wait(act, s["u_ready"], i - 1)
            for n in range(2):
                A(conv[par][:, n, :], pair0[:, n, :], ACT.Identity, bias=consts["conv_b"][:, n:n + 1],
                  scale=consts["conv_w"][:, n, TAPS - 1:TAPS]).then_inc(s["conv_init"], 1)
        if live(i, -2):
            b = i - 2
            wait(act, s["mg_ps"], b + 1)
            wait(act, s["shrink_ps"], b)
            A(grown, pair1[:, :, :], ACT.Gelu).then_inc(s["mg_ready"], 1)
        if live(i, 0):
            wait(act, s["gate_ps"], i + 1)
            wait(act, s["gh_ready"], i - 1)
            A(gate_g[par], pair0[:, :, :], ACT.Gelu).then_inc(s["gate_ready"], 1)
        if live(i, -1):
            b = i - 1
            wait(act, s["om_ready"], b + 1)
            A(beta, beta, ACT.Sqrt, bias=consts["tiny"][:, 0:1]).then_inc(s["beta_ready"], 1)
        if live(i, -3):
            b = i - 3
            wait(act, s["h4T_ps"], b + 1)
            wait(act, s["y_ps"], b)
            A(h4T, bank_t[:, :], ACT.Copy).then_inc(s["h4T_ready"], 1)

    def vector(dve, i, par):
        TT, TS, STT = nc.vector.tensor_tensor, nc.vector.tensor_scalar, nc.vector.scalar_tensor_tensor
        chunk = lambda x: (lambda c: x[:, c * D:(c + 1) * D])
        x_chunk = lambda b: (lambda c: x_all[:, b, c * D:(c + 1) * D])
        par1 = (par + 1) & 1

        def raw(which, name, src):
            raw_stats(nc, stats[which][0], src, s[f"stat_{name}_raw"], C)

        def aggregate(which, name, b):
            mean_var(nc, dve, *stats[which], s[f"stat_{name}_raw"], s[f"stat_{name}"], C, b, past_wait)

        def scaled(dst, src, mv, r, done):
            for c in range(C):
                TS(dst[:, c * D:(c + 1) * D], src(c), mv[:, c, 0:1], r[:, c:c + 1], ALU.subtract, ALU.mult)\
                    .then_inc(done, 1)

        if live(i, 1):
            b = i + 1
            wait(dve, sems["x2_step"], 10 * (b + 1))
            wait(dve, s["xn_ready"], b - 1)
            raw(f"x2_{par1}", "x2", x_chunk(b))
            aggregate(f"x2_{par1}", "x2", b)
        if live(i, -4):
            b = i - 4
            wait(dve, s["y_ps"], b + 1)
            wait(dve, s["yc_ready"], b)
            TT(y.rearrange("p (c d) -> p c d", c=C), bank_y[:, :].rearrange("p (c d) -> p c d", c=C),
               consts["b_expert"][:, :].unsqueeze(1).to_broadcast([P, C, D]), ALU.add).then_inc(s["y_ready"], 1)
            q = s["top_step"]
            wait(dve, s["logits_ps"], b + 1)
            nc.vector.tensor_reduce(top[:, 0, :], log_ps.rearrange("p (c e) -> p c e", e=E), AX_X, ALU.max)\
                .then_inc(q, 1)
            wait(dve, s["y_ready"], b + 1)
            raw("y", "y", chunk(y))
            wait(dve, q, 2 * b + 1)
            wait(dve, s["route_step"], 8 * b)
            wait(dve, s["exps_ready"], b)
            TT(shifted[:, :, :], log_ps.rearrange("p (c e) -> p c e", e=E),
               top[:, 0, :].unsqueeze(2).to_broadcast([P, C, E]), ALU.subtract).then_inc(q, 1)
            aggregate("y", "y", b)
        if live(i, -4):
            b = i - 4
            q, at = s["route_step"], 8 * b
            wait(dve, s["top_step"], 2 * (b + 1))
            STT(ranked[:, :, :], shifted[:, :, :], 0.0, consts["rev"][:, :, :], ALU.is_ge, ALU.mult).then_inc(q, 1)
            wait(dve, q, at + 1)
            nc.vector.tensor_reduce(top[:, 1, :], ranked[:, :, :], AX_X, ALU.max).then_inc(q, 1)
            wait(dve, q, at + 2)
            wait(dve, s["cum_ready"], b)
            wait(dve, s["place_step"], 3 * b)
            TT(chosen[:, :, :], consts["rev"][:, :, :], top[:, 1, :].unsqueeze(2).to_broadcast([P, C, E]),
               ALU.is_equal).then_inc(q, 1)
        if live(i, -2):
            b = i - 2
            wait(dve, s["wout_ps"], b + 1)
            wait(dve, s["z3_ready"], C * (b + 1))
            TT(zx[par], zx[par], bank_o[:, :], ALU.add).then_inc(s["xh_ready"], 1)
            wait(dve, s["xh_ready"], b + 1)
            wait(dve, s["rs_h_step"], 3 * b)
            raw("h", "h", chunk(zx[par]))
            aggregate("h", "h", b)
        if live(i, -3):
            b = i - 3
            wait(dve, s["shrink_ps"], b + 1)
            wait(dve, s["x3_ready"], b)
            TT(t, zx[par1], bank_y[:, :], ALU.add).then_inc(s["t_ready"], 1)
            wait(dve, s["t_ready"], b + 1)
            raw("t", "t", chunk(t))
        if live(i, -4):
            b = i - 4
            q, at = s["route_step"], 8 * b
            wait(dve, s["exps_ready"], b + 1)
            nc.vector.tensor_reduce(top[:, 2, :], exps[:, :, :], AX_X, ALU.add).then_inc(q, 1)
        if live(i, -3):
            aggregate("t", "t", i - 3)
        if live(i, -4):
            b = i - 4
            q, at = s["route_step"], 8 * b
            wait(dve, q, at + 4)
            nc.vector.reciprocal(top[:, 3, :], top[:, 2, :]).then_inc(q, 1)
        if live(i, -4):
            b = i - 4
            q, at = s["route_step"], 8 * b
            wait(dve, q, at + 5)
            TT(top[:, 4, :], top[:, 3, :], top[:, 3, :], ALU.mult).then_inc(q, 1)
        if live(i, -4):
            b = i - 4
            q, at = s["route_step"], 8 * b
            wait(dve, q, at + 6)
            wait(dve, s["stat_y"], C * (b + 1))
            TT(top[:, 5, :], top[:, 4, :], stats["y"][1][:, :, 1], ALU.mult).then_inc(q, 1)
            qc, atc = s["count_step"], 2 * b
            wait(dve, qc, atc)
            nc.vector.tensor_reduce(counted[:, :], chosen[:, :, :].rearrange("p c e -> p e c"), AX_X, ALU.add)\
                .then_inc(qc, 1)
            wait(dve, q, at + 7)
            wait(dve, s["rs_y_step"], 2 * b)
            TS(rs["y"][:, 0, :], top[:, 5, :], EPS, None, ALU.add).then_inc(q, 1)
        if live(i, -3):
            b = i - 3
            wait(dve, s["rs_t_step"], 2 * (b + 1))
            scaled(t, chunk(t), stats["t"][1], rs["t"][:, 1, :], s["tn_ready"])
        if live(i, -1):
            b = i - 1
            wait(dve, s["inp_tanh"], 2 * (b + 1))
            STT(inp, inp, 1.0, conv[par1], ALU.add, ALU.mult).then_inc(s["u_ready"], 1)
        if live(i, -3):
            b = i - 3
            wait(dve, s["x3_ready"], b + 1)
            raw("x3", "x3", x_chunk(b))
        if live(i, -4):
            b = i - 4
            q, at = s["place_step"], 3 * b
            wait(dve, s["cum_ready"], b + 1)
            TT(placed[:, :, :], chosen[:, :, :], cum_ps.rearrange("p (c e) -> p c e", e=E), ALU.mult).then_inc(q, 1)
        if live(i, -3):
            aggregate("x3", "x3", i - 3)
        if live(i, -4):
            b = i - 4
            q, at = s["place_step"], 3 * b
            wait(dve, q, at + 1)
            nc.vector.tensor_reduce(top[:, 6, :], placed[:, :, :], AX_X, ALU.add).then_inc(q, 1)
            wait(dve, s["count_step"], 2 * b + 1)
            TT(counts[:, :], counts[:, :], counted[:, :], ALU.add).then_inc(s["count_step"], 1)
            wait(dve, q, at + 2)
            wait(dve, s["rs_y_step"], 2 * b)
            STT(top[:, 7, :], top[:, 6, :], float(CAPACITY), top[:, 3, :], ALU.is_le, ALU.mult).then_inc(q, 1)

        def taps(which):
            q, at = s["conv_step"], 2 * (TAPS - 1) * i
            for tap in which:
                if tap == 0:
                    wait(dve, s["xc_copied"], i + 1)
                    wait(dve, s["conv_init"], 2 * (i + 1))
                else:
                    wait(dve, q, at + 2 * tap)
                for n in range(2):
                    STT(conv[par][:, n, :], xc_pad[:, n, tap:tap + T], consts["conv_w"][:, n, tap:tap + 1],
                        conv[par][:, n, :], ALU.mult, ALU.add).then_inc(q, 1)

        def normed_x3():
            b = i - 3
            wait(dve, s["rs_x3_step"], 2 * (b + 1))
            wait(dve, s["h4T_ps"], b)
            scaled(h4, x_chunk(b), stats["x3"][1], rs["x3"][:, 1, :], s["h4_ready"])
        if live(i, 0):
            taps(range(0, 1))
        if live(i, -3):
            normed_x3()
        if live(i, 0):
            taps(range(1, TAPS - 1))
        if live(i, -1):
            b = i - 1
            wait(dve, s["u_ready"], b + 1)
            wait(dve, s["beta_ready"], b + 1)
            STT(inp, inp, 0.5, beta, ALU.mult, ALU.mult).then_inc(s["xs_ready"], 1)
            wait(dve, s["xs_ready"], b + 1)
            wait(dve, s["gh_ready"], b)
            for n in range(2):
                nc.vector.tensor_tensor_scan(h[:, n, :], alpha[:, n, :], inp[:, n, :], 0.0, ALU.mult, ALU.add)\
                    .then_inc(s["h_ready"], 1)
        if live(i, -2):
            b = i - 2
            wait(dve, s["mx_ps"], b + 1)
            wait(dve, s["mg_ready"], b + 1)
            TT(grown, grown, pair1[:, :, :], ALU.mult).then_inc(s["grown_ready"], 1)

    def pool(gp, i, par):
        TT, TS = nc.gpsimd.tensor_tensor, nc.gpsimd.tensor_scalar
        half_neg = consts["pow"][:, 0, :]
        per_token = lambda x: x.unsqueeze(2).to_broadcast([P, C, D])
        rows = lambda x: x.rearrange("p (c d) -> p c d", c=C)

        def rsqrt(name, b):
            q, mv, r = s[f"rs_{name}_step"], stats[name][1], rs[name]
            wait_apart(gp, s[f"stat_{name}"], C * (b + 1), past_wait)
            TS(r[:, 0, :], mv[:, :, 1], EPS, None, ALU.add).then_inc(q, 1)
            wait_apart(gp, q, 2 * b + 1, past_wait)
            TT(r[:, 1, :], r[:, 0, :], half_neg, ALU.pow).then_inc(q, 1)

        if live(i, 0):
            b = i
            q, mv, r = s["rs_x2_step"], stats[f"x2_{par}"][1], rs_x2[par]
            wait_apart(gp, s["stat_x2"], C * (b + 1), past_wait)
            wait_apart(gp, s["z3_ready"], C * (b - 1), past_wait)
            TT(r[:, 2, :], mv[:, :, 1], half_neg, ALU.pow).then_inc(q, 1)
            TS(r[:, 0, :], mv[:, :, 1], EPS, None, ALU.add).then_inc(q, 1)
            TT(r[:, 3, :], mv[:, :, 0], consts["pow"][:, 2, :], ALU.mult).then_inc(q, 1)
            wait_apart(gp, s["xT_ps"], b, past_wait)
            TT(rows(xn), rows(x_all[:, b, :]), per_token(mv[:, :, 0]), ALU.subtract).then_inc(s["xn_step"], 1)
            wait_apart(gp, q, 5 * b + 3, past_wait)
            TT(r[:, 1, :], r[:, 0, :], half_neg, ALU.pow).then_inc(q, 1)
            wait_apart(gp, s["xn_step"], b + 1, past_wait)
            TT(rows(xn), rows(xn), per_token(r[:, 2, :]), ALU.mult).then_inc(s["xn_ready"], 1)
            wait_apart(gp, q, 5 * b + 4, past_wait)
            TT(r[:, 3, :], r[:, 3, :], r[:, 1, :], ALU.mult).then_inc(q, 1)
        if live(i, -2):
            b = i - 2
            q, mv, r = s["rs_h_step"], stats["h"][1], rs["h"]
            wait_apart(gp, s["stat_h"], C * (b + 1), past_wait)
            TT(r[:, 0, :], mv[:, :, 0], mv[:, :, 0], ALU.mult).then_inc(q, 1)
            wait_apart(gp, q, 3 * b + 1, past_wait)
            TT(r[:, 1, :], r[:, 0, :], mv[:, :, 1], ALU.add).then_inc(q, 1)
            wait_apart(gp, q, 3 * b + 2, past_wait)
            TT(r[:, 2, :], r[:, 1, :], half_neg, ALU.pow).then_inc(q, 1)
            wait_apart(gp, q, 3 * b + 3, past_wait)
            wait_apart(gp, s["xn2T_ps"], b, past_wait)
            TT(rows(xn2), rows(zx[par]), per_token(r[:, 2, :]), ALU.mult).then_inc(s["xn2_ready"], 1)
        if live(i, -3):
            rsqrt("t", i - 3)
        if live(i, -1):
            b = i - 1
            wait_apart(gp, s["sq_ready"], b + 1, past_wait)
            TS(beta, beta, -1.0, 1.0, ALU.mult, ALU.add).then_inc(s["om_ready"], 1)
        if live(i, -3):
            b = i - 3
            wait_apart(gp, s["tn_ready"], C * (b + 1), past_wait)
            TT(x_all[:, b, :], x_all[:, b, :], t, ALU.add).then_inc(s["x3_ready"], 1)
        if live(i, -3):
            rsqrt("x3", i - 3)
        if live(i, -4):
            b = i - 4
            wait_apart(gp, s["route_step"], 8 * (b + 1), past_wait)
            TT(rs["y"][:, 1, :], rs["y"][:, 0, :], half_neg, ALU.pow).then_inc(s["rs_y_step"], 1)
            wait_apart(gp, s["x4_ready"], b, past_wait)
            TT(rows(acc_y), rows(y), per_token(stats["y"][1][:, :, 0]), ALU.subtract).then_inc(s["yc_ready"], 1)
        if live(i, -4):
            b = i - 4
            wait_apart(gp, s["place_step"], 3 * (b + 1), past_wait)
            wait_apart(gp, s["rs_y_step"], 2 * b + 1, past_wait)
            TT(rs["y"][:, 2, :], rs["y"][:, 1, :], top[:, 7, :], ALU.mult).then_inc(s["rs_y_step"], 1)
            wait_apart(gp, s["yc_ready"], b + 1, past_wait)
            wait_apart(gp, s["rs_y_step"], 2 * (b + 1), past_wait)
            TT(rows(acc_y), rows(acc_y), per_token(rs["y"][:, 2, :]), ALU.mult).then_inc(s["yn_ready"], 1)
            wait_apart(gp, s["yn_ready"], b + 1, past_wait)
            TT(x_all[:, b, :], x_all[:, b, :], acc_y, ALU.add).then_inc(s["x4_ready"], 1)
        if live(i, -1):
            b = i - 1
            wait_apart(gp, s["h_ready"], 2 * (b + 1), past_wait)
            wait_apart(gp, s["gate_ready"], b + 1, past_wait)
            wait_apart(gp, s["wout_ps"], b, past_wait)
            TT(gh, h, gate_g[(par + 1) & 1], ALU.mult).then_inc(s["gh_ready"], 1)

    def first_half(eng):
        wait(eng, sems["pv_done"], 16 * NB - 4)

    def all_free(eng):
        wait(eng, sems["pv_done"], 16 * NB)
        wait(eng, sems["max_read"], 32 * NB)
        wait(eng, sems["exp_done"], 64 * NB)
        wait(eng, sems["acc_read"], 2 * NB)

    def begin(eng, step, which):
        for i in which:
            step(eng, i, i % 2)

    def iterate(eng, step):
        for i in range(2, 6):
            step(eng, i, i % 2)
        with eng.Fori(0, (NB - 8) // 2) as k:
            step(eng, k * 2 + 6, 0)
            step(eng, k * 2 + 7, 1)
        for i in range(NB - 2, NB + 4):
            step(eng, i, i % 2)

    def store(sp, stored):
        with sp.Fori(0, NB) as b:
            wait_apart(sp, s["x4_ready"], b + 1, past_wait)
            sp.dma_start(out[b].rearrange("(c p) d -> p c d", p=P),
                         x_all[:, b, :].rearrange("p (c d) -> p c d", c=C)).then_inc(stored, 16)
        sp.wait_ge(stored, 16 * NB)

    return {"tensor": tensor, "scalar": scalar, "vector": vector, "pool": pool, "store": store,
            "first_half": first_half, "all_free": all_free, "begin": begin, "iterate": iterate, "counts": counts, "xc_pad": xc_pad}


def build(nc, a, out):
    x_in = a["z"]
    NB, T = x_in.shape[0], x_in.shape[1]
    C = T // P
    E = a["w_gate"].shape[1]

    with ExitStack() as ctx:
        def sb(name, shape, dt=F32):
            return ctx.enter_context(nc.sbuf_tensor(name, shape, dt))

        def sem(name):
            return ctx.enter_context(nc.semaphore(name))

        psum = [ctx.enter_context(nc.psum_tensor(f"bank_pair{i}", [P, 2, T], F32)) for i in range(2)]
        psum += [ctx.enter_context(nc.psum_tensor(f"bank{i}", [P, T], F32)) for i in range(4)]
        x_all = sb("x_all", [P, NB, C * D])
        w = {"q": sb("w_q", [P, P]), "k": sb("w_k", [P, P]), "v": sb("w_v", [P, P]), "proj": sb("w_proj", [P, P]),
             "ffn": sb("w_ffn", [P, P], BF16)}
        w.update({"in": sb("w_in", [P, 1, 4 * P]), "gates": sb("w_gates", [P, 2, 4 * P]), "out": sb("w_out", [P, 2, P]),
                  "grow": sb("w_grow", [P, 1, 4 * P]), "shrink": sb("w_shrink", [P, 2, P]),
                  "route": sb("w_route", [P, E]), "expert": sb("w_expert", [P, P])})
        consts = {"ident": sb("ident", [P, P]), "ident_bf": sb("ident_bf", [P, P], BF16),
                  "pow": sb("pow", [P, 3, C]), "b_proj": sb("b_proj", [P, D]), "ffn_bias": sb("ffn_bias", [P, D], BF16),
                  "ln_scale": sb("ln_scale", [P, 1]), "ln_bias": sb("ln_bias", [P, 1]),
                  "s_in": sb("s_in", [P, 1]), "s_k": sb("s_k", [P, 1]), "s_in_inv": sb("s_in_inv", [P, 1]),
                  "s_k_inv": sb("s_k_inv", [P, 1]), "s_both": sb("s_both", [P, 1])}
        consts.update({"tri": sb("tri", [P, P], BF16), "ones": sb("ones", [P, P], BF16), "rev": sb("rev", [P, C, E]),
                       "conv_w": sb("conv_w", [P, 2, 4]), "conv_b": sb("conv_b", [P, 2]), "b_half": sb("b_half", [P, 4]),
                       "k_half": sb("k_half", [P, 2]), "gamma1": sb("gamma1", [P, 1]), "gamma2": sb("gamma2", [P, 1]),
                       "b_expert": sb("b_expert", [P, D]), "tiny": sb("tiny_c", [P, 1])})
        tri_raw = sb("tri_raw", [P, P])
        b_gates = sb("b_gates", [P, 4])
        soft = sb("soft", [P, 8, 2])
        ffn_raw = sb("ffn_raw", [P, D], BF16)
        loaded, pool_set, dve_set, dve_const = sem("loaded"), sem("pool_set"), sem("dve_set"), sem("dve_const")
        out_done = sem("out_done")
        sems = {"x_loaded": sem("x_loaded"), "past_wait": sem("past_wait")}
        att = attention_phase(nc, ctx, sems, psum, x_in, x_all, w, consts, NB)

        layer1 = hawk_moe_phase(nc, ctx, sems, psum, x_all, att["probs"],
                                att["v_pad"][0][:, :, :, :].rearrange("p c h e -> p (c h e)"),
                                att["zn"][:, :, :].rearrange("p c d -> p (c d)"), w, consts, out, NB, T)
        soft_step, loaded1, pool_set1, pads_set = sem("soft_step"), sem("loaded1"), sem("pool_set1"), sem("pads_set")

        ffn_scaled, ffn_grid, ffn_under, ffn_over = (att["probs"][:, n, 0:D] for n in range(4))

        loads = [(w[n][:, :], a["w_" + n]) for n in ("q", "k", "v", "proj")]
        loads += [(ffn_raw[:, :], a["ffn_kernel"])]
        loads += [(consts[n][:, :], a[n].rearrange("(p a) -> p a", a=1)) for n in ("ln_scale", "ln_bias")]
        loads += [(consts[n][:, :], a[n].rearrange("(a d) -> a d", a=1).to_broadcast([P, a[n].shape[0]]))
                  for n in ("b_proj", "ffn_bias", "s_in", "s_k")]
        loads1 = [(w["in"][:, 0, :], a["w_in"]), (w["gates"][:, :, :], a["w_gates"].rearrange("(k p) n -> p k n", p=P)),
                  (w["out"][:, :, :], a["w_out"].rearrange("(k p) n -> p k n", p=P)), (w["grow"][:, 0, :], a["w_grow"]),
                  (w["shrink"][:, :, :], a["w_shrink"].rearrange("(k p) n -> p k n", p=P)),
                  (w["route"][:, :], a["w_gate"]), (w["expert"][:, :], a["w_expert"]),
                  (consts["conv_w"][:, :, :], a["conv_w"]), (consts["conv_b"][:, :], a["conv_b"]),
                  (b_gates[:, :], a["b_gates"]), (soft[:, 0, :], a["forget_base"]),
                  (consts["b_expert"][:, :], a["b_expert"].rearrange("(a d) -> a d", a=1).to_broadcast([P, D]))]
        loads1 += [(consts[n][:, :], a[n].rearrange("(p a) -> p a", a=1)) for n in ("gamma1", "gamma2")]
        LOADED1, POOL_SET1 = 16 * len(loads1), 5 + E
        TERMS = 8
        SOFT = 8 + TERMS
        LOADED, POOL_SET, DVE_SET, PADS_SET = 16 * len(loads), 5, 10, 6

        block = ctx.enter_context(nc.Block())

        @block.sync
        def _(sp):
            for dst, src in loads:
                sp.dma_start(dst, src).then_inc(loaded, 16)
            for dst, src in loads1:
                sp.dma_start(dst, src).then_inc(loaded1, 16)
            sp.wait_ge(pads_set, PADS_SET)
            att["iterate"](sp, att["sync"])
            for i in (NB, NB + 1):
                att["tail"](sp, att["sync"], i)
            layer1["store"](sp, out_done)

        @block.gpsimd
        def _(gp):
            ident = consts["ident"]
            nc.gpsimd.memset(ident[:, :], 0.0).then_inc(pool_set, 1)
            for n, v in enumerate((-0.5, 0.5, -1.0)):
                nc.gpsimd.memset(consts["pow"][:, n, :], v).then_inc(pool_set, 1)
            gp.wait_ge(pool_set, 1)
            nc.gpsimd.affine_select(out=ident[:, :], in_=ident[:, :], compare_op=ALU.not_equal, fill=1.0, base=0,
                                    pattern=[[-1, P]], channel_multiplier=1).then_inc(pool_set, 1)
            gp.wait_ge(dve_set, DVE_SET)
            gp.wait_ge(pads_set, PADS_SET)
            gp.wait_ge(pool_set, POOL_SET)
            nc.gpsimd.memset(tri_raw[:, :], 1.0).then_inc(pool_set1, 1)
            gp.wait_ge(pool_set1, 1)
            nc.gpsimd.affine_select(out=tri_raw[:, :], in_=tri_raw[:, :], compare_op=ALU.is_ge, fill=0.0, base=0,
                                    pattern=[[1, P]], channel_multiplier=-1).then_inc(pool_set1, 1)
            nc.gpsimd.memset(consts["ones"][:, :], 1.0).then_inc(pool_set1, 1)
            nc.gpsimd.memset(consts["tiny"][:, :], 1e-6).then_inc(pool_set1, 1)
            nc.gpsimd.memset(layer1["counts"][:, :], 0.0).then_inc(pool_set1, 1)
            for e in range(E):
                nc.gpsimd.memset(consts["rev"][:, :, e:e + 1], float(E - e)).then_inc(pool_set1, 1)
            att["iterate"](gp, att["pool"])
            layer1["first_half"](gp)
            nc.gpsimd.memset(layer1["xc_pad"][:, :, 0:3], 0.0).then_inc(pool_set1, 1)
            layer1["begin"](gp, layer1["pool"], range(-1, 1))
            att["tail"](gp, att["pool"], NB)
            layer1["all_free"](gp)
            layer1["begin"](gp, layer1["pool"], range(1, 2))
            att["tail"](gp, att["pool"], NB + 1)
            layer1["iterate"](gp, layer1["pool"])

        @block.vector
        def _(dve):
            TS = nc.vector.tensor_scalar
            for stack in att["k_stacks"]:
                nc.vector.memset(stack[:, :, :], 1.0).then_inc(pads_set, 1)
            for v in att["v_pad"]:
                nc.vector.memset(v[:, :, :, :], 0.0).then_inc(pads_set, 1)
            dve.wait_ge(pads_set, 4)
            for v in att["v_pad"]:
                dst = v[:, :, :, :].rearrange("p c (u t g) e -> p (c u) t g e", u=2, t=2)
                for t in range(2):
                    last = nc.vector.memset(dst[:, :, t, :, 16 * t + 8:16 * t + 9], 1.0)
                last.then_inc(pads_set, 1)
            dve.wait_ge(loaded, LOADED)
            nc.vector.reciprocal(consts["s_in_inv"][:, :], consts["s_in"][:, :]).then_inc(dve_set, 1)
            nc.vector.reciprocal(consts["s_k_inv"][:, :], consts["s_k"][:, :]).then_inc(dve_set, 1)
            nc.vector.tensor_tensor(consts["s_both"][:, :], consts["s_in"][:, :], consts["s_k"][:, :], ALU.mult)\
                .then_inc(dve_set, 1)
            dve.wait_ge(pool_set, POOL_SET)
            nc.vector.tensor_copy(consts["ident_bf"][:, :], consts["ident"][:, :]).then_inc(dve_set, 1)
            dve.wait_ge(dve_set, 2)
            TS(ffn_scaled, ffn_raw[:, :], consts["s_k_inv"][:, 0:1], None, ALU.mult).then_inc(dve_set, 1)
            dve.wait_ge(dve_set, 5)
            TS(ffn_grid.bitcast(U32), ffn_scaled.bitcast(U32), 0x7F800000, None, ALU.bitwise_and)\
                .then_inc(dve_set, 1)
            TS(ffn_over, ffn_scaled, 464.0, 464.0, ALU.max, ALU.subtract).then_inc(dve_const, 1)
            TS(ffn_under, ffn_scaled, -464.0, 464.0, ALU.min, ALU.add).then_inc(dve_const, 1)
            dve.wait_ge(dve_const, 2)
            nc.vector.tensor_tensor(ffn_over, ffn_over, ffn_under, ALU.subtract)\
                .then_inc(dve_const, 1)
            dve.wait_ge(dve_const, 3)
            TS(ffn_over, ffn_over, 1e30, 1e30, ALU.mult, ALU.mult).then_inc(dve_const, 1)
            dve.wait_ge(dve_const, 4)
            TS(ffn_over, ffn_over, 1e30, None, ALU.mult).then_inc(dve_const, 1)
            dve.wait_ge(dve_set, 6)
            TS(ffn_grid, ffn_grid, 2.0 ** -6, 1.5 * 2.0 ** 20, ALU.max, ALU.mult).then_inc(dve_set, 1)
            dve.wait_ge(dve_set, 7)
            nc.vector.tensor_tensor(ffn_scaled, ffn_scaled, ffn_grid, ALU.add).then_inc(dve_set, 1)
            dve.wait_ge(dve_set, 8)
            nc.vector.tensor_tensor(ffn_scaled, ffn_scaled, ffn_grid, ALU.subtract)\
                .then_inc(dve_set, 1)
            dve.wait_ge(dve_set, 9)
            dve.wait_ge(dve_const, 5)
            nc.vector.tensor_tensor(w["ffn"][:, :], ffn_scaled, ffn_over, ALU.add).then_inc(dve_set, 1)
            dve.wait_ge(dve_set, DVE_SET)
            att["iterate"](dve, att["vector"])
            dve.wait_ge(loaded1, LOADED1)
            layer1["first_half"](dve)
            layer1["begin"](dve, layer1["vector"], range(-1, 0))
            q = soft_step
            dve.wait_ge(pool_set1, POOL_SET1)
            row = lambda n: soft[:, n, :]
            TS(row(1), row(0), -1.0, None, ALU.mult).then_inc(q, 1)
            dve.wait_ge(q, 1)
            nc.vector.tensor_tensor(row(1), row(0), row(1), ALU.max).then_inc(q, 1)
            TS(row(6), row(0), 0.0, -4.0, ALU.max, ALU.mult).then_inc(q, 1)
            dve.wait_ge(q, 4)
            TS(row(3), row(2), 2.0, None, ALU.add).then_inc(q, 1)
            dve.wait_ge(q, 5)
            nc.vector.reciprocal(row(3), row(3)).then_inc(q, 1)
            dve.wait_ge(q, 6)
            nc.vector.tensor_tensor(row(3), row(2), row(3), ALU.mult).then_inc(q, 1)
            dve.wait_ge(q, 7)
            nc.vector.tensor_tensor(row(4), row(3), row(3), ALU.mult).then_inc(q, 1)
            dve.wait_ge(q, 8)
            TS(row(5), row(4), 1.0 / (2 * TERMS - 1), None, ALU.mult).then_inc(q, 1)
            for n in range(TERMS - 2, 0, -1):
                dve.wait_ge(q, 7 + TERMS - n)
                nc.vector.scalar_tensor_tensor(row(5), row(5), 1.0 / (2 * n + 1), row(4), ALU.add, ALU.mult)\
                    .then_inc(q, 1)
            dve.wait_ge(q, 7 + TERMS)
            nc.vector.scalar_tensor_tensor(row(5), row(5), 1.0, row(3), ALU.add, ALU.mult).then_inc(q, 1)
            dve.wait_ge(q, SOFT)
            nc.vector.scalar_tensor_tensor(consts["k_half"][:, :], row(5), -8.0, row(6), ALU.mult, ALU.add)\
                .then_inc(q, 1)
            TS(consts["b_half"][:, :], b_gates[:, :], 0.5, None, ALU.mult).then_inc(q, 1)
            nc.vector.tensor_copy(consts["tri"][:, :], tri_raw[:, :]).then_inc(q, 1)
            att["tail"](dve, att["vector"], NB)
            dve.wait_ge(pool_set1, POOL_SET1 + 1)
            layer1["all_free"](dve)
            layer1["begin"](dve, layer1["vector"], range(0, 2))
            att["tail"](dve, att["vector"], NB + 1)
            layer1["iterate"](dve, layer1["vector"])

        @block.scalar
        def _(act):
            act.wait_ge(loaded, LOADED)
            act.wait_ge(dve_set, DVE_SET)
            act.wait_ge(pads_set, PADS_SET)
            act.wait_ge(pool_set, POOL_SET)
            att["iterate"](act, att["scalar"])
            act.wait_ge(soft_step, 3)
            nc.scalar.activation(soft[:, 2, :], soft[:, 1, :], ACT.Exp, scale=-1.0).then_inc(soft_step, 1)
            att["tail"](act, att["scalar"], NB)
            act.wait_ge(soft_step, SOFT + 3)
            layer1["all_free"](act)
            act.wait_ge(loaded1, LOADED1)
            layer1["begin"](act, layer1["scalar"], range(-1, 2))
            att["tail"](act, att["scalar"], NB + 1)
            layer1["iterate"](act, layer1["scalar"])

        @block.tensor
        def _(pe):
            pe.wait_ge(loaded, LOADED)
            pe.wait_ge(dve_set, DVE_SET)
            pe.wait_ge(pads_set, PADS_SET)
            pe.wait_ge(pool_set, POOL_SET)
            att["iterate"](pe, att["tensor"])
            att["tail"](pe, att["tensor"], NB)
            layer1["all_free"](pe)
            pe.wait_ge(loaded1, LOADED1)
            pe.wait_ge(soft_step, SOFT + 3)
            layer1["begin"](pe, layer1["tensor"], range(-1, 2))
            att["tail"](pe, att["tensor"], NB + 1)
            wait(pe, sems["ffn_read"], NB)
            layer1["iterate"](pe, layer1["tensor"])


def layouts(i):
    import numpy as np
    D = 128
    qkv = np.asarray(i["L0_attn_w_qkv"]).reshape(D, 8, 2, 8, 3)
    a = {"z": i["L0_attn_z"]}
    a["w_q"] = qkv[..., 0].transpose(0, 2, 3, 1).reshape(D, D)
    a["w_k"] = qkv[..., 1].transpose(0, 2, 3, 1).reshape(D, D)
    a["w_v"] = qkv[..., 2].reshape(D, D)
    a["w_proj"] = np.asarray(i["L0_attn_w_proj"]).reshape(2, 2, 4, 8, D).transpose(0, 2, 1, 3, 4).reshape(D, D)
    L1 = {n[8:]: np.asarray(v) for n, v in i.items() if n.startswith("L1_attn_")}
    for n in ("W_in", "W_gates", "W_out", "W_grow", "W_shrink"):
        a[n.lower()] = L1[n].T
    a["conv_w"] = L1["conv_w"].reshape(2, D, 4).transpose(1, 0, 2)
    for n in ("conv_b", "b_gates", "forget_base"):
        a[n] = L1[n].reshape(-1, D).T
    a["gamma1"], a["gamma2"] = L1["gamma1"], L1["gamma2"]
    for n in ("w_gate", "w_expert", "b_expert"):
        a[n] = i["L1_ffn_" + n]
    for new, old in (("ln_scale", "L0_attn_ln_scale"), ("ln_bias", "L0_attn_ln_bias"), ("b_proj", "L0_attn_b_proj"),
                     ("ffn_kernel", "L0_ffn_kernel"), ("s_in", "L0_ffn_input_scale"), ("s_k", "L0_ffn_kernel_scale"),
                     ("ffn_bias", "L0_ffn_bias")):
        a[new] = i[old]
    return {n: np.ascontiguousarray(v) for n, v in a.items()}


def kernel(**inputs):
    import concourse.bacc as bacc
    from concourse.bass_utils import run_bass_kernel_spmd

    nc = bacc.Bacc("TRN2", target_bir_lowering=False, num_devices=1)
    arrays = layouts(inputs)
    aps = {n: nc.dram_tensor(f"in_{n}_dram", v.shape, mybir.dt.from_np(v.dtype), kind="ExternalInput").ap()
           for n, v in arrays.items()}
    out = nc.dram_tensor("out_0_dram", arrays["z"].shape, F32, kind="ExternalOutput").ap()
    build(nc, aps, out)
    r = run_bass_kernel_spmd(nc, [{f"in_{n}_dram": v for n, v in arrays.items()}], core_ids=[0])
    return r.results[0]["out_0_dram"]
```
